# Optimizing a Trainium2 kernel written in Bass

```python
import numpy as np
import jax
import jax.numpy as jnp

def _softmax(x, axis=-1):
    return jax.nn.softmax(x, axis=axis)

def _gelu(x):
    return jax.nn.gelu(x, approximate=True)

def _silu(x):
    return jax.nn.silu(x)

def _sigmoid(x):
    return jax.nn.sigmoid(x)

def _layernorm(x, axis=-1, eps=1e-05):
    m = jnp.mean(x, axis=axis, keepdims=True)
    v = jnp.var(x, axis=axis, keepdims=True)
    return (x - m) / jnp.sqrt(v + eps)

def _scatter_add(tgt, idx, src, axis=0):
    return tgt.at[idx].add(src)

def _segment_sum(src, seg, n):
    return jax.ops.segment_sum(src, seg, n)
kernel_name = 'mk_decoder_postln_d1_seqx_r4_fb9617'

def setup_inputs(seed: int=0):
    np.random.seed(seed)
    _w = jnp.asarray

    def _rec_inputs():
        import jax
        import jax.numpy as jnp
        _rk = jax.random.key(seed)
        x = -0.0002928 + 1 * jax.random.normal(jax.random.fold_in(_rk, 1), (8, 256, 512), jnp.float32)
        _lenS = 256 - jax.random.randint(jax.random.fold_in(_rk, 7), (8,), 0, max(1, 256 // 4) + 1, jnp.int32)
        _lenS2 = 256 - jax.random.randint(jax.random.fold_in(_rk, 8), (8,), 0, max(1, 256 // 4) + 1, jnp.int32)
        _ctx_2048P = jax.random.normal(jax.random.fold_in(_rk, 11), (8, 16, 512), jnp.float32)
        _ctx_2048c = jax.random.dirichlet(jax.random.fold_in(_rk, 511), 0.3 * jnp.ones((16,), jnp.float32), (8, 256))
        _ctx_2048t = jnp.einsum('bsk,bkd->bsd', _ctx_2048c, _ctx_2048P)
        _ctx_2048t = _ctx_2048t * jax.lax.rsqrt(jnp.mean(jnp.square(_ctx_2048t)) + 1e-12) * 0.953939
        ctx_2048 = -1.39393e-06 + 0.999914 * (_ctx_2048t + 0.3 * jax.random.normal(jax.random.fold_in(_rk, 611), (8, 256, 512), jnp.float32))
        return (x, ctx_2048)
    x, ctx_2048 = _rec_inputs()

    def _L0_attn_setup():
        import jax, jax.numpy as jnp
        import numpy as np
        NUM_HEADS = 16
        CHUNK = 128

        def _bitlinear(x, w, b):
            w_scale = jnp.maximum(jnp.mean(jnp.abs(w)), 1e-05)
            w_norm = w / w_scale
            w_q = jax.lax.stop_gradient(jnp.sign(w_norm) - w_norm) + w_norm
            x_scale = jnp.maximum(jnp.max(jnp.abs(x), axis=-1, keepdims=True), 1e-05)
            x_norm = x / x_scale * 127.0
            x_q = jax.lax.stop_gradient(jnp.round(x_norm) - x_norm) + x_norm
            return jnp.einsum('...i,oi->...o', x_q, w_q) * (x_scale * w_scale / 127.0) + b

        def _rmsnorm(x, w, eps=1e-06):
            return x * jax.lax.rsqrt(jnp.mean(x * x, axis=-1, keepdims=True) + eps) * w
        key = jax.random.key(seed)
        ks = jax.random.split(key, 8)
        B, N, C = (2, 1024, 512)

        def w(k, shape):
            return jax.random.normal(k, shape, jnp.float32) * 0.02
        return {'x': jax.random.normal(ks[0], (B, N, C), jnp.float32), 'qkv_w': w(ks[1], (3 * C, C)), 'qkv_b': w(ks[2], (3 * C,)), 'gate_w': w(ks[3], (C, C)), 'gate_b': w(ks[4], (C,)), 'proj_w': w(ks[5], (C, C)), 'proj_b': w(ks[6], (C,)), 'norm_w': jnp.ones((C,), jnp.float32)}
    _L0_attn_all = _L0_attn_setup()
    _L0_attn_in = {k: v for k, v in _L0_attn_all.items() if k in ('qkv_w', 'qkv_b', 'gate_w', 'gate_b', 'proj_w', 'proj_b', 'norm_w')}
    del _L0_attn_all

    def _L0_xattn_setup():
        import jax, jax.numpy as jnp
        import numpy as np
        HID = 512
        H = 32
        HK = 8
        G = H // HK
        D = HID // H
        T = 256
        W_ATT = 64
        W_SSM = 64

        def _heads(x, n):
            B, Tt, _ = x.shape
            return x.reshape(B, Tt, n, D).transpose(0, 2, 1, 3)

        def _attend(q, k, v):
            pos = jnp.arange(T)
            rel = pos[None, :] - pos[:, None]
            slopes = jnp.power(2.0, -8.0 * jnp.arange(H, dtype=jnp.float32) / H)
            alibi = slopes[:, None, None] * rel.astype(jnp.float32)
            bias = jnp.concatenate([alibi, alibi], axis=-1)
            delta = -rel
            ssm_mask = (delta >= 0) & (delta < W_SSM)
            att_mask = (delta >= 0) & (delta < W_ATT)
            mask = jnp.concatenate([ssm_mask, att_mask], axis=-1)
            scores = jnp.einsum('bhqd,bhkd->bhqk', q, k) / np.sqrt(D).astype(np.float32)
            scores = scores + bias[None]
            scores = jnp.where(mask[None, None], scores, -jnp.inf)
            wei = jax.nn.softmax(scores, axis=-1)
            return jnp.einsum('bhqk,bhkd->bhqd', wei, v)
        key = jax.random.key(seed)
        ks = jax.random.split(key, 8)
        s = lambda fan_in: 1.0 / np.sqrt(fan_in)
        return {'hidden_states': jax.random.normal(ks[0], (2, T, HID), jnp.float32), 'ssm_states': jax.random.normal(ks[1], (2, T, HID), jnp.float32), 'Wq': jax.random.normal(ks[2], (2 * HID, HID), jnp.float32) * s(2 * HID), 'Wk': jax.random.normal(ks[3], (HID, HK * D), jnp.float32) * s(HID), 'Wv': jax.random.normal(ks[4], (HID, HK * D), jnp.float32) * s(HID), 'Wsk': jax.random.normal(ks[5], (HID, HK * D), jnp.float32) * s(HID), 'Wsv': jax.random.normal(ks[6], (HID, HK * D), jnp.float32) * s(HID), 'Wo': jax.random.normal(ks[7], (HID, HID), jnp.float32) * s(HID)}
    _L0_xattn_all = _L0_xattn_setup()
    _L0_xattn_in = {k: v for k, v in _L0_xattn_all.items() if k in ('Wq', 'Wk', 'Wv', 'Wsk', 'Wsv', 'Wo')}
    del _L0_xattn_all

    def _L0_ffn_setup():
        import jax, jax.numpy as jnp
        import numpy as np
        B, S, D_IN, D_OUT, E, R = (4, 512, 512, 512, 8, 16)
        SCALING = 32.0 / 16.0
        key = jax.random.key(seed)
        ks = jax.random.split(key, 7)
        return {'x': jax.random.normal(ks[0], (B, S, D_IN), jnp.float32), 'base_w': jax.random.normal(ks[1], (D_OUT, D_IN), jnp.float32) * 0.02, 'base_b': jax.random.normal(ks[2], (D_OUT,), jnp.float32) * 0.02, 'router_w': jax.random.normal(ks[3], (E, D_IN), jnp.float32) * 0.02, 'router_b': jax.random.normal(ks[4], (E,), jnp.float32) * 0.02, 'lora_A': jax.random.normal(ks[5], (E, D_IN, R), jnp.float32) * 0.02, 'lora_B': jax.random.normal(ks[6], (E, R, D_OUT), jnp.float32) * 0.02}
    _L0_ffn_all = _L0_ffn_setup()
    _L0_ffn_in = {k: v for k, v in _L0_ffn_all.items() if k in ('base_w', 'base_b', 'router_w', 'router_b', 'lora_A', 'lora_B')}
    del _L0_ffn_all
    return {'x': x, 'ctx_2048': ctx_2048, 'L0_attn_qkv_w': _L0_attn_in['qkv_w'], 'L0_attn_qkv_b': _L0_attn_in['qkv_b'], 'L0_attn_gate_w': _L0_attn_in['gate_w'], 'L0_attn_gate_b': _L0_attn_in['gate_b'], 'L0_attn_proj_w': _L0_attn_in['proj_w'], 'L0_attn_proj_b': _L0_attn_in['proj_b'], 'L0_attn_norm_w': _L0_attn_in['norm_w'], 'L0_xattn_Wq': _L0_xattn_in['Wq'], 'L0_xattn_Wk': _L0_xattn_in['Wk'], 'L0_xattn_Wv': _L0_xattn_in['Wv'], 'L0_xattn_Wsk': _L0_xattn_in['Wsk'], 'L0_xattn_Wsv': _L0_xattn_in['Wsv'], 'L0_xattn_Wo': _L0_xattn_in['Wo'], 'L0_ffn_base_w': _L0_ffn_in['base_w'], 'L0_ffn_base_b': _L0_ffn_in['base_b'], 'L0_ffn_router_w': _L0_ffn_in['router_w'], 'L0_ffn_router_b': _L0_ffn_in['router_b'], 'L0_ffn_lora_A': _L0_ffn_in['lora_A'], 'L0_ffn_lora_B': _L0_ffn_in['lora_B']}

def reference(x, ctx_2048, L0_attn_qkv_w, L0_attn_qkv_b, L0_attn_gate_w, L0_attn_gate_b, L0_attn_proj_w, L0_attn_proj_b, L0_attn_norm_w, L0_xattn_Wq, L0_xattn_Wk, L0_xattn_Wv, L0_xattn_Wsk, L0_xattn_Wsv, L0_xattn_Wo, L0_ffn_base_w, L0_ffn_base_b, L0_ffn_router_w, L0_ffn_router_b, L0_ffn_lora_A, L0_ffn_lora_B):
    import jax
    import jax.numpy as jnp

    def _L0_attn_ref(x, qkv_w, qkv_b, gate_w, gate_b, proj_w, proj_b, norm_w):
        import jax, jax.numpy as jnp
        import numpy as np
        NUM_HEADS = 16
        CHUNK = 128

        def _bitlinear(x, w, b):
            w_scale = jnp.maximum(jnp.mean(jnp.abs(w)), 1e-05)
            w_norm = w / w_scale
            w_q = jax.lax.stop_gradient(jnp.sign(w_norm) - w_norm) + w_norm
            x_scale = jnp.maximum(jnp.max(jnp.abs(x), axis=-1, keepdims=True), 1e-05)
            x_norm = x / x_scale * 127.0
            x_q = jax.lax.stop_gradient(jnp.round(x_norm) - x_norm) + x_norm
            return jnp.einsum('...i,oi->...o', x_q, w_q) * (x_scale * w_scale / 127.0) + b

        def _rmsnorm(x, w, eps=1e-06):
            return x * jax.lax.rsqrt(jnp.mean(x * x, axis=-1, keepdims=True) + eps) * w
        B, N, C = x.shape
        H, L = (NUM_HEADS, CHUNK)
        D = C // H
        scale = D ** (-0.5)
        qkv = _bitlinear(x, qkv_w, qkv_b).reshape(B, N, 3, H, D)
        q, k, v = (qkv[:, :, 0], qkv[:, :, 1], qkv[:, :, 2])
        g = jax.nn.sigmoid(_bitlinear(x, gate_w, gate_b)).reshape(B, N, H, D)
        nc = N // L

        def chunks(t):
            return t.reshape(B, nc, L, H, D).transpose(1, 0, 2, 3, 4)
        qc, kc, vc, gc = map(chunks, (q, k, v, g))

        def step(kv_state, inp):
            qi, ki, vi, gi = inp
            attn = jax.nn.softmax(jnp.einsum('blhd,blgd->blhg', qi, ki) * scale, axis=-1)
            local = jnp.einsum('blhg,blgd->blhd', attn, vi)
            recur = jnp.einsum('blhd,bhde->blhe', qi, kv_state)
            decay = jnp.mean(gi, axis=1)[..., None]
            kv_update = jnp.einsum('blhd,blhe->bhde', ki, vi)
            return (kv_state * decay + kv_update, local + recur)
        kv0 = jnp.zeros((B, H, D, D), x.dtype)
        _, out = jax.lax.scan(step, kv0, (qc, kc, vc, gc))
        out = out.transpose(1, 0, 2, 3, 4).reshape(B, N, C)
        return _bitlinear(_rmsnorm(out, norm_w), proj_w, proj_b)

    def _L0_xattn_ref(hidden_states, ssm_states, Wq, Wk, Wv, Wsk, Wsv, Wo):
        import jax, jax.numpy as jnp
        import numpy as np
        HID = 512
        H = 32
        HK = 8
        G = H // HK
        D = HID // H
        T = 256
        W_ATT = 64
        W_SSM = 64

        def _heads(x, n):
            B, Tt, _ = x.shape
            return x.reshape(B, Tt, n, D).transpose(0, 2, 1, 3)

        def _attend(q, k, v):
            pos = jnp.arange(T)
            rel = pos[None, :] - pos[:, None]
            slopes = jnp.power(2.0, -8.0 * jnp.arange(H, dtype=jnp.float32) / H)
            alibi = slopes[:, None, None] * rel.astype(jnp.float32)
            bias = jnp.concatenate([alibi, alibi], axis=-1)
            delta = -rel
            ssm_mask = (delta >= 0) & (delta < W_SSM)
            att_mask = (delta >= 0) & (delta < W_ATT)
            mask = jnp.concatenate([ssm_mask, att_mask], axis=-1)
            scores = jnp.einsum('bhqd,bhkd->bhqk', q, k) / np.sqrt(D).astype(np.float32)
            scores = scores + bias[None]
            scores = jnp.where(mask[None, None], scores, -jnp.inf)
            wei = jax.nn.softmax(scores, axis=-1)
            return jnp.einsum('bhqk,bhkd->bhqd', wei, v)
        B = hidden_states.shape[0]
        q = _heads(jnp.concatenate([ssm_states, hidden_states], axis=-1) @ Wq, H)
        k = _heads(hidden_states @ Wk, HK)
        v = _heads(hidden_states @ Wv, HK)
        ssm_k = _heads(ssm_states @ Wsk, HK)
        ssm_v = _heads(ssm_states @ Wsv, HK)
        rep = lambda x: jnp.repeat(x, G, axis=1)
        kcat = jnp.concatenate([rep(ssm_k), rep(k)], axis=2)
        vcat = jnp.concatenate([rep(ssm_v), rep(v)], axis=2)
        o = _attend(q, kcat, vcat)
        o = o.transpose(0, 2, 1, 3).reshape(B, T, HID)
        return o @ Wo

    def _L0_ffn_ref(x, base_w, base_b, router_w, router_b, lora_A, lora_B):
        import jax, jax.numpy as jnp
        import numpy as np
        B, S, D_IN, D_OUT, E, R = (4, 512, 512, 512, 8, 16)
        SCALING = 32.0 / 16.0
        b, s, d_in = x.shape
        n = b * s
        e = lora_A.shape[0]
        d_out = lora_B.shape[-1]
        result = jnp.einsum('bsd,od->bso', x, base_w) + base_b
        logits = jnp.einsum('bsd,ed->bse', x, router_w) + router_b
        probs = jax.nn.softmax(logits.astype(jnp.float32), axis=-1)
        top_vals, top_idx = jax.lax.top_k(probs, 2)
        top_vals = top_vals / jnp.sum(top_vals, axis=-1, keepdims=True)
        top_vals = top_vals.astype(x.dtype)
        flat_idx = top_idx.reshape(n, 2)
        flat_val = top_vals.reshape(n, 2)
        gate = jnp.zeros((n, e), x.dtype).at[jnp.arange(n)[:, None], flat_idx].set(flat_val)
        xf = x.reshape(n, d_in)
        mid = jnp.einsum('nd,edr->ner', xf, lora_A)
        mid = mid * gate[:, :, None]
        lora_out = jnp.einsum('ner,erd->nd', mid, lora_B)
        return result + SCALING * lora_out.reshape(b, s, d_out)
    x = _layernorm(x + _L0_attn_ref(x, L0_attn_qkv_w, L0_attn_qkv_b, L0_attn_gate_w, L0_attn_gate_b, L0_attn_proj_w, L0_attn_proj_b, L0_attn_norm_w), axis=-1)
    x = _layernorm(x + _L0_xattn_ref(x, ctx_2048, L0_xattn_Wq, L0_xattn_Wk, L0_xattn_Wv, L0_xattn_Wsk, L0_xattn_Wsv, L0_xattn_Wo), axis=-1)
    x = _layernorm(x + _L0_ffn_ref(x, L0_ffn_base_w, L0_ffn_base_b, L0_ffn_router_w, L0_ffn_router_b, L0_ffn_lora_A, L0_ffn_lora_B), axis=-1)
    return x

_drawn_inputs = setup_inputs


def setup_inputs(seed=0):
    import zlib

    import numpy as np

    out = dict(_drawn_inputs(seed))
    spreads = {'L0_attn_norm_w': (1.0, 0.2)}
    factors = {'L0_attn_proj_b': 2.808, 'L0_ffn_base_b': 3.17, 'L0_ffn_router_b': 6.094}
    for name, (base, spread) in spreads.items():
        noise = np.random.default_rng([zlib.crc32(name.encode()), seed]).standard_normal(out[name].shape)
        drawn = base * np.exp(spread * noise) if base else spread * noise
        out[name] = jnp.asarray(drawn.astype(out[name].dtype))
    for name, factor in factors.items():
        out[name] = (out[name] * factor).astype(out[name].dtype)
    return out
```

```python
from contextlib import ExitStack

import numpy as np

import concourse.bass as bass
from concourse import mybir

F32 = mybir.dt.float32
BF16 = mybir.dt.bfloat16
ALU = mybir.AluOpType
ACT = mybir.ActivationFunctionType
AX = mybir.AxisListType

P = 128
S = 32
NB, N, C = 8, 256, 512
T = N // P
KT = C // P
HA, DA = 16, 32
HT = P // DA
TOK = P // HA
GRP = P // TOK
HB, KVB, DB = 32, 8, 16
G = HB // KVB
WIN = 64
QB = N // S
KB = N // (2 * S)
E, R = 8, 16
SCALING = 2.0
W_LOADS = 8 + 4 + KVB + KT
BIG = -1.0e30
MAGIC = 12582912.0
EPS_RMS, EPS_LN = 1e-6, 1e-5


def constants():
    f = {}
    f["eye"] = np.eye(P)
    f["ones"] = np.ones((P, P))
    f["ramp"] = np.broadcast_to(np.arange(E, 0, -1.0), (P, E))
    f["strip"] = np.repeat(np.eye(HT), S, axis=0)
    f["neghalf"] = np.full((P, 2), -0.5)
    b = {}
    b["eye"] = np.eye(P)
    tok = np.arange(P) // HA
    sel = np.zeros((P, GRP, P))
    for p in range(3):
        for j in range(GRP):
            sel[p * GRP + j, j, :] = 1
    for r in range(TOK):
        sel[3 * GRP + r, :, :] = tok == r
    b["sel"] = sel.reshape(P, -1)
    low = np.zeros((P, P))
    for r in range(TOK):
        low[3 * GRP + r] = np.where(tok == r, 0.0, BIG)
    b["maxt0"] = low
    tokhot, other = np.zeros((P, P)), np.zeros((P, 4, P))
    for r in range(TOK):
        tokhot[r] = tok == r
        other[r] = np.where(tok == r, 0.0, BIG)
    b["tokhot"], b["other"] = tokhot, other.reshape(P, -1)
    rep = np.zeros((P, P))
    for q in range(S):
        rep[q, q::S] = 1
    b["rep"] = rep
    q, k = np.arange(S)[:, None], np.arange(S)[None, :]
    m = np.zeros((P, 2, 2, S))
    m[:S, 0] = np.where(k > q, 0.0, BIG)[:, None]
    m[:S, 1] = np.where(k <= q, 0.0, BIG)[:, None]
    b["mask_nat"] = m.reshape(P, -1)
    key = np.zeros((P, 2, 2, S))
    for r in range(2 * S):
        key[r, r // S, :, r % S] = 1
    b["key"] = key.reshape(P, -1)
    r = np.arange(2 * S)[:, None, None, None]
    qq = (np.arange(4)[:, None, None] * S + np.arange(S)[None, None, :])[None]
    ok = np.broadcast_to((qq - r >= 0) & (qq - r < WIN), (2 * S, 4, G, S))
    m = np.zeros((P, 4 * P))
    m[:2 * S] = np.where(ok, 0.0, BIG).reshape(2 * S, -1)
    b["mask_tr"] = m
    slope = (np.power(np.float32(2.0), (-8.0 * np.arange(HB, dtype=np.float32) / HB)) * np.float32(DB ** 0.5)).astype(np.float32)
    trunc = lambda v: (v.astype(np.float32).view(np.uint32) & 0xFFFF0000).view(np.float32)
    s1 = trunc(slope); s2 = trunc(slope - s1); s3 = slope - s1 - s2
    qx = np.zeros((HB, S)); qx[:, 3], qx[:, 4], qx[:, 5] = s1, s2, s3
    b["qx"] = np.broadcast_to(qx[None], (P, HB, S)).reshape(P, -1)
    kx = np.zeros((P, T, S)); kx[:, :, 0:3] = 1
    for t in range(T):
        kx[:, t, 3:6] = (np.arange(P) + P * t - N // 2)[:, None]
    b["kx"] = kx.reshape(P, -1)
    def pack(d):
        at, cols = {}, 0
        for name, a in d.items():
            at[name] = (cols, a.shape[1]); cols += a.shape[1]
        return at, np.concatenate(list(d.values()), axis=1).astype(np.float32)
    return pack(f), pack(b)


def program(nc, d, out):
    (f_at, f_arr), (b_at, b_arr) = constants()
    ctx = ExitStack()
    with ctx:
        def sb(name, shape, dt=F32):
            return ctx.enter_context(nc.sbuf_tensor(name, shape, dt))

        class Signal:

            def __init__(self, name, per):
                self.sem = ctx.enter_context(nc.semaphore(name))
                self.per = per

            def upto(self, b, k=None):
                return self.per * b + (self.per if k is None else k)

            def __call__(self, eng, b, k=None):
                eng.wait_ge(self.sem, self.upto(b, k))

            def before(self, eng, b):
                if not (isinstance(b, int) and b == 0):
                    eng.wait_ge(self.sem, self.per * b)

        class Chain:

            def __init__(self, name, per):
                self.s = Signal(name, per)
                self.k = 0

            def start(self, eng, b):
                self.eng, self.b, self.k = eng, b, 0

            def link(self, ins):
                self.k += 1
                ins.then_inc(self.s.sem, 1)
                self.eng.wait_ge(self.s.sem, self.s.per * self.b + self.k)

            def end(self):
                assert self.k == self.s.per, (self.k, self.s.per)

        cf = sb("cf", [P, f_arr.shape[1]])
        cb = sb("cb", [P, b_arr.shape[1]], BF16)
        fc = lambda n: cf[:, f_at[n][0]:f_at[n][0] + f_at[n][1]]
        bc = lambda n: cb[:, b_at[n][0]:b_at[n][0] + b_at[n][1]]
        eye, ones, ramp, strip, neghalf = fc("eye"), fc("ones"), fc("ramp"), fc("strip"), fc("neghalf")
        eyeb, rep, key, mask_tr = bc("eye"), bc("rep"), bc("key"), bc("mask_tr")
        sel = bc("sel").rearrange("p (h g) -> p h g", h=GRP)
        tokhot, other = bc("tokhot"), bc("other")
        mask_nat = bc("mask_nat").rearrange("p (r k) -> p r k", r=2)
        qx = bc("qx").rearrange("p (h c) -> p h c", h=HB)
        kx = bc("kx").rearrange("p (t c) -> p t c", t=T)

        qkv_sign = sb("qkv_sign", [P, KT, 3 * C], BF16)
        proj_sign = sb("proj_sign", [P, KT, C], BF16)
        base_t = sb("base_t", [P, KT, C])
        wq = sb("wq", [P, 2 * KT, C])
        wkv = sb("wkv", [P, 4, KT, P])
        wo = sb("wo", [P, G, C])
        rl = sb("rl", [P, KT, E + P])
        lora_b = sb("lora_b", [P, C])
        qkv_bias = sb("qkv_bias", [P, 3 * C])
        proj_bias = sb("proj_bias", [P, C])
        norm_w = sb("norm_w", [P, C])
        base_bias = sb("base_bias", [P, C])
        router_bias = sb("router_bias", [P, E])
        abs_sums = sb("abs_sums", [P, 4])
        wscale = sb("wscale", [P, 4])

        x_in = sb("x_in", [P, T, C])
        x_res = sb("x_res", [P, T, C])
        xq = sb("xq", [P, T, C], BF16)
        xq_t = sb("xq_t", [P, KT, N], BF16)
        st_a = sb("st_a", [P, 8, T])
        nat = sb("nat", [P, T, 3, C])
        y_a = nat[:, :, 1, :]
        q_t = sb("q_t", [P, KT, P])
        k8 = sb("k8", [P, T, S, HA])
        q_bd = sb("q_bd", [P, 4, HT, P])
        v8t = [nat[:, t, t, :].rearrange("p (j d) -> p j d", j=GRP) for t in range(T)]
        kv_bd = sb("kv_bd", [P, KT, P])
        p_a = sb("p_a", [P, HA, P])
        max_a = sb("max_a", [P, 3, HA])
        maxp_a = sb("maxp_a", [P, 3, HA], BF16)
        maxt_a = sb("maxt_a", [P, P], BF16)
        sum_a = sb("sum_a", [P, HA, DA])
        v8 = sum_a[:, :, :].rearrange("p a b -> p (a b)").rearrange("p (n h) -> p n h", h=HA)
        rinv_a = sb("rinv_a", [P, HA])
        out_a = sb("out_a", [P, T, C])
        q8 = out_a[:, :, :].rearrange("p t (n h) -> p t n h", h=HA)
        stats = sb("stats", [P, T, 6])
        mv_a = sb("mv_a", [P, T, 2])
        rs_a = sb("rs_a", [P, 4, T])
        x1 = sb("x1", [P, T, C])
        x1_t = sb("x1_t", [P, KT, N])

        c_in = sb("c_in", [P, T, C])
        p_b = sb("p_b", [P, 2, 4, 4 * P])
        flat = p_b[:, :, :, :].rearrange("p a b c -> p (a b c)")
        c_t = flat[:, 0:KT * N].rearrange("p (k n) -> p k n", k=KT)
        kn = flat[:, KT * N:2 * KT * N].bitcast(BF16).rearrange("p (s g c) -> p s g c", s=2, g=KVB)
        qn = flat[:, 2 * KT * N:4 * KT * N].bitcast(BF16).rearrange("p (h c) -> p h c", h=HB)
        q_rest = c_in[:, 0, :]
        k_rest = c_in[:, 1, 0:2 * P]
        qt_b = sb("qt_b", [P, QB, KVB, P], BF16)
        kt_b = sb("kt_b", [P, KVB, QB, 2 * S], BF16)
        v_b = sb("v_b", [P, KB, KVB, S])
        max_b = sb("max_b", [P, 2, QB, KVB])
        maxp_b = sb("maxp_b", [P, 2, 3, QB // 2, KVB], BF16)
        maxt_b = sb("maxt_b", [3 * S, 2, P], BF16)
        o_tb = c_in[:, :, :].rearrange("p a (b c) -> p (a b) c", c=P)
        rinv_b = sb("rinv_b", [P, QB, 4])
        qflat = qt_b[:, :, :, :].rearrange("p a b c -> p (a b c)").bitcast(F32)
        on_b = qflat[:, 0:QB * P].rearrange("p (i g d) -> p i g d", i=QB, g=KVB)
        o_fb = qflat[:, QB * P:QB * P + G * N].rearrange("p (h n) -> p h n", h=G)
        mv_b = sb("mv_b", [P, T, 2])
        rs_b = sb("rs_b", [P, 2, T])
        x2 = sb("x2", [P, T, C])
        router_nat = x2[0:E, 0, :]
        x2_t = sb("x2_t", [P, KT, N])

        g_c = sb("g_c", [P, 12, T, E])
        gs_c = sb("gs_c", [P, 6, T])
        gm = sb("gm", [P, T, P])
        gm_t = sb("gm_t", [P, T, P])
        mv_c = sb("mv_c", [P, T, 2])
        rs_c = sb("rs_c", [P, 2, T])
        z_c = x2

        ps = ctx.enter_context(nc.psum_tensor("ps", [P, 8, 512], F32))
        bank = lambda k: ps[:, k, :]
        bankb = lambda k: ps[:, k, :].bitcast(BF16)

        raw = [p_b[:, n, :, :] for n in range(2)]
        qt_flat = qt_b[:, :, :, :].rearrange("p a b c -> p (a b c)")
        sgn = [qt_flat[:, n * KT * C:(n + 1) * KT * C]
               .rearrange("p (a b) -> p a b", a=KT) for n in range(2)]

        const_in = Signal("const_in", 0)
        raw_in = [Signal(f"raw_in{n}", 0) for n in range(2)]
        rout_in = Signal("rout_in", 0)
        w_in = Signal("w_in", 0)
        zeroed = Signal("zeroed", 0)
        signed = Signal("signed", 0)
        summed = Signal("summed", 0)
        turned = Signal("turned", 0)
        kept = Signal("kept", 0)
        total = Signal("total", 0)
        scaled = Signal("scaled", 0)

        x_here = Signal("x_here", 16)
        x_scaled = Signal("x_scaled", 1)
        x_kept = Signal("x_kept", 1)
        a_max = Signal("a_max", 1)
        x_round = Signal("x_round", 1)
        xq_turn = Signal("xq_turn", 1)
        xq_here = Signal("xq_here", 1)
        qkv_full = Signal("qkv_full", 6)
        nat_here = Signal("nat_here", 6)
        t8_here = Signal("t8_here", 6)
        vt_turn = Signal("vt_turn", 2)
        vt_here = Signal("vt_here", 2)
        qt_turn = Signal("qt_turn", 1)
        qt_here = Signal("qt_here", 1)
        bd_here = Signal("bd_here", 2)
        kv_full = Signal("kv_full", 1)
        kv_here = Signal("kv_here", 1)
        s_full = Signal("s_full", 2)
        s_max = Signal("s_max", 2)
        m_parts = Signal("m_parts", 2)
        m_turn = Signal("m_turn", 2)
        m_here = Signal("m_here", 2)
        st_full = Signal("st_full", 8)
        pa_here = Signal("pa_here", 8)
        oa_full = Signal("oa_full", 2)
        rec_full = Signal("rec_full", 1)
        outa_here = Signal("outa_here", 2)
        sq_here = Signal("sq_here", 2)
        ms_here = Signal("ms_here", 1)
        rms_here = Signal("rms_here", 1)
        b_max = Signal("b_max", 1)
        o_scaled = Signal("o_scaled", 1)
        o_round = Signal("o_round", 1)
        oq_turn = Signal("oq_turn", 1)
        oq_here = Signal("oq_here", 1)
        pr_full = Signal("pr_full", 2)
        za_here = Signal("za_here", 2)
        va_here = Signal("va_here", 1)
        ra_here = Signal("ra_here", 1)
        x1_here = Signal("x1_here", 2)
        x1_turn = Signal("x1_turn", 2)
        x1t_here = Signal("x1t_here", 2)

        c_here = Signal("c_here", 16)
        c_turn = Signal("c_turn", 2)
        ct_here = Signal("ct_here", 2)
        v_full = Signal("v_full", 1)
        v_here = Signal("v_here", 1)
        q_full = Signal("q_full", 4)
        q_first = Signal("q_first", 4)
        q_read = Signal("q_read", 4)
        q_slots = Signal("q_slots", 4)
        qb_turn = Signal("qb_turn", 12)
        qb_act = Signal("qb_act", 8)
        kb_dve = Signal("kb_dve", 4)
        sb_full = Signal("sb_full", 16)
        sb_max = Signal("sb_max", 16)
        mb_parts = Signal("mb_parts", 1)
        mb_turn = Signal("mb_turn", 1)
        mb_here = Signal("mb_here", 1)
        mb_sent = Signal("mb_sent", 16 * 6)
        stb_full = Signal("stb_full", 32)
        pb_here = Signal("pb_here", 32)
        pv_done = Signal("pv_done", 8)
        ob_here = Signal("ob_here", 2)
        ob_turn = Signal("ob_turn", 2)
        on_here = Signal("on_here", 2)
        of_turn = Signal("of_turn", 1)
        of_here = Signal("of_here", 1)
        wo_full = Signal("wo_full", 2)
        zb_here = Signal("zb_here", 2)
        vb_here = Signal("vb_here", 1)
        rb_here = Signal("rb_here", 1)
        x2_here = Signal("x2_here", 2)
        x2_turn = Signal("x2_turn", 2)
        x2t_here = Signal("x2t_here", 2)

        rl_full = Signal("rl_full", 1)
        lg_here = Signal("lg_here", 1)
        ex_here = Signal("ex_here", 1)
        gm_here = Signal("gm_here", 1)
        gm_turn = Signal("gm_turn", 1)
        gmt_here = Signal("gmt_here", 1)
        x2_kept = Signal("x2_kept", 1)
        ff_full = Signal("ff_full", 2)
        zc_here = Signal("zc_here", 2)
        vc_here = Signal("vc_here", 1)
        rc_here = Signal("rc_here", 1)
        y_here = Signal("y_here", 1)
        y_sent = Signal("y_sent", 16)
        tmpa = Signal("tmpa", 1)
        out1 = Signal("out1", 1)
        g1 = Signal("g1", 3)

        carry = {n: ctx.enter_context(nc.semaphore("carry_" + n)) for n in ("pe", "dve", "pool")}

        def carried(eng, n):
            eng.sem_inc(carry[n], 1)

        ch = {n: Chain("ch_" + n, k) for n, k in dict(a1=2, a2=12, a3=4, a4=3, b1=4, b2=3, b3=2, b4=3, c1=15, c2=3).items()}

        block = ctx.enter_context(nc.Block())
        xv = d["x"].rearrange("b (t p) c -> b p t c", p=P)
        cv = d["ctx_2048"].rearrange("b (t p) c -> b p t c", p=P)
        ov = out.rearrange("b (t p) c -> b p t c", p=P)
        one = lambda v, b: v[bass.ds(b, 1), :, :, :].rearrange("a p t c -> p (a t) c")

        NEXT, A, B, C_ = -1, 0, 1, 2

        def run(eng, stages):
            def step(i):
                for lag, stage in stages:
                    if not isinstance(i, int) or 0 <= i - lag < NB:
                        stage(i - lag)

            for i in range(-1, 2):
                step(i)
            with eng.Fori(2, NB - 1) as i:
                step(i)
            for i in range(NB - 1, NB + 2):
                step(i)

        @block.sync
        def _(sp):
            sp.dma_start(cf[:, :], d["const_f"]).then_inc(const_in.sem, 16)
            pieces = [d["L0_attn_qkv_w"][n * C:(n + 1) * C, :] for n in range(3)] + [d["L0_attn_proj_w"], d["L0_ffn_base_w"]]
            for n, w in enumerate(pieces):
                if n >= 2:
                    sp.wait_ge(signed.sem, n - 1)
                    sp.wait_ge(summed.sem, n - 1)
                sp.dma_start(raw[n % 2], w.rearrange("(a p) c -> p a c", p=P)).then_inc(raw_in[n % 2].sem, 16)
                if n == 1:
                    sp.dma_start(router_nat[:, :], d["L0_ffn_router_w"]).then_inc(rout_in.sem, 16)
            row = lambda a: a.rearrange("(a n) -> a n", a=1)
            loads = [
                (qkv_bias[:, :], row(d["L0_attn_qkv_b"]).to_broadcast([P, 3 * C])),
                (proj_bias[:, :], row(d["L0_attn_proj_b"]).to_broadcast([P, C])),
                (norm_w[:, :], row(d["L0_attn_norm_w"]).to_broadcast([P, C])),
                (base_bias[:, :], row(d["L0_ffn_base_b"]).to_broadcast([P, C])),
                (router_bias[:, :], row(d["L0_ffn_router_b"]).to_broadcast([P, E])),
                (wq[:, :, :], d["L0_xattn_Wq"].rearrange("(k p) n -> p k n", p=P)),
                (lora_b[:, :], d["L0_ffn_lora_B"].rearrange("e r n -> (e r) n")),
            ]
            loads.append((maxt_a[:, :], d["const_b"][:, b_at["maxt0"][0]:b_at["maxt0"][0] + P]))
            for n, w in enumerate(("Wsk", "Wk", "Wsv", "Wv")):
                loads.append((wkv[:, n, :, :], d["L0_xattn_" + w].rearrange("(k p) n -> p k n", p=P)))
            for k in range(KVB):
                loads.append((wo[k * DB:(k + 1) * DB, :, :],
                              d["L0_xattn_Wo"][k * G * DB:(k + 1) * G * DB, :].rearrange("(h d) n -> d h n", d=DB)))
            for k in range(KT):
                loads.append((rl[:, k, E:].rearrange("p (e r) -> p e r", e=E),
                              d["L0_ffn_lora_A"][:, k * P:(k + 1) * P, :].rearrange("e p r -> p e r")))
            assert len(loads) == W_LOADS
            for dst, src in loads:
                sp.dma_start(dst, src).then_inc(w_in.sem, 16)

            def a0(b):
                x_kept.before(sp, b)
                x_scaled.before(sp, b)
                a_max.before(sp, b)
                sp.dma_start(x_in[:, :, :], one(xv, b)).then_inc(x_here.sem, 16)

            def b1(b):
                ob_turn.before(sp, b)
                sp.dma_start(c_in[:, :, :], one(cv, b)).then_inc(c_here.sem, 16)

            def b2(b):
                mb_here(sp, b)
                sb_max(sp, b)
                for half in range(2):
                    for p in range(3):
                        sp.dma_start(
                            qt_b[96 + p:97 + p, half * 4:half * 4 + 4, :, :].rearrange("p i g q -> p (i g) q"),
                            maxt_b[p * S:(p + 1) * S, half, :]).then_inc(mb_sent.sem, 16)

            def c2(b):
                y_here(sp, b)
                sp.dma_start(one(ov, b), z_c[:, :, :]).then_inc(y_sent.sem, 16)

            run(sp, [(NEXT, a0), (B, b2), (C_, c2), (A, b1)])
            y_sent(sp, NB - 1)

        W_IN = 16 * W_LOADS

        @block.gpsimd
        def _(pool):
            pool.memset(kv_bd[:, :, :], 0.0).then_inc(zeroed.sem, 1)
            pool.memset(v_b[:, :, :, :], 0.0).then_inc(zeroed.sem, 1)
            pool.wait_ge(zeroed.sem, 2)
            pool.memset(v_b[:, :, :, DB:DB + 1], 1.0).then_inc(zeroed.sem, 1)
            pool.wait_ge(zeroed.sem, 3)
            pool.wait_ge(w_in.sem, W_IN)
            pool.wait_ge(const_in.sem, 32)

            def a0(b):
                a_max(pool, b)
                x_here(pool, b)
                x_round.before(pool, b)
                o_round.before(pool, b)
                carried(pool, "pool")
                for t in range(T):
                    ins = pool.tensor_scalar(y_a[:, t, :], x_in[:, t, :], st_a[:, 1, t:t + 1], 127.0, ALU.mult, ALU.mult)
                ins.then_inc(x_scaled.sem, 1)

            def a1(b):
                za_here.before(pool, b)
                for t in range(T):
                    ins = pool.tensor_tensor(x_res[:, t, :], x_in[:, t, :], proj_bias[:, :], ALU.add)
                ins.then_inc(x_kept.sem, 1)
                for t in range(T):
                    t8_here(pool, b, 3 * t + 1)
                    if t:
                        st_full(pool, b, 4)
                    else:
                        st_full.before(pool, b)
                    carried(pool, "pool")
                    for s in range(HT):
                        ins = pool.tensor_scalar(q_bd[:, :, s, :], q8[:, t, :, :].rearrange("p (c n) h -> p c (n h)", c=4), strip[:, s:s + 1], 1.0, ALU.mult, ALU.mult)
                    ins.then_inc(bd_here.sem, 1)

            def a3(b):
                ms_here(pool, b)
                pool.tensor_tensor(rs_a[:, 1, :], rs_a[:, 0, :], neghalf, ALU.pow).then_inc(rms_here.sem, 1)
                b_max(pool, b)
                x_round(pool, b)
                carried(pool, "pool")
                for t in range(T):
                    ins = pool.tensor_scalar(y_a[:, t, :], out_a[:, t, :], st_a[:, 5, t:t + 1], 127.0, ALU.mult, ALU.mult)
                ins.then_inc(o_scaled.sem, 1)

            def a4(b):
                va_here(pool, b)
                pool.tensor_tensor(rs_a[:, 3, :], rs_a[:, 2, :], neghalf, ALU.pow).then_inc(ra_here.sem, 1)

            def b4(b):
                vb_here(pool, b)
                pool.tensor_tensor(rs_b[:, 1, :], rs_b[:, 0, :], neghalf, ALU.pow).then_inc(rb_here.sem, 1)

            def c1(b):
                x2_turn(pool, b)
                for t in range(T):
                    ins = pool.tensor_tensor(z_c[:, t, :], x2[:, t, :], base_bias[:, :], ALU.add)
                ins.then_inc(x2_kept.sem, 1)

            def c2(b):
                vc_here(pool, b)
                pool.tensor_tensor(rs_c[:, 1, :], rs_c[:, 0, :], neghalf, ALU.pow).then_inc(rc_here.sem, 1)

            run(pool, [(A, a1), (C_, c1), (A, a3), (C_, c2), (A, a4), (NEXT, a0), (B, b4)])

        @block.scalar
        def _(act):
            act.dma_start(cb[:, :], d["const_b"]).then_inc(const_in.sem, 16)
            for n in range(4):
                act.wait_ge(raw_in[n % 2].sem, 16 * (n // 2 + 1))
                if n >= 2:
                    act.wait_ge(turned.sem, n - 1)
                act.activation(sgn[n % 2], raw[n % 2], ACT.Sign).then_inc(signed.sem, 1)
            for n in range(3):
                act.wait_ge(turned.sem, n + 1)
                act.activation(qkv_sign[:, :, n * C:(n + 1) * C].rearrange("p k (j o) -> p k j o", j=4),
                               ps[:, 2 * n:2 * n + 2, :].bitcast(BF16).rearrange("p b (k j o) -> p (b k) j o", k=2, j=4),
                               ACT.Copy).then_inc(kept.sem, 1)
            act.wait_ge(turned.sem, 4)
            act.activation(proj_sign[:, :, :].rearrange("p k (j o) -> p k j o", j=4),
                           ps[:, 6:8, :].bitcast(BF16).rearrange("p b (k j o) -> p (b k) j o", k=2, j=4),
                           ACT.Copy).then_inc(kept.sem, 1)
            act.wait_ge(turned.sem, 5)
            act.activation(base_t[:, :, :], ps[:, 0:4, :], ACT.Copy).then_inc(kept.sem, 1)
            act.activation(rl[:, :, 0:E], ps[:, 4, 0:KT * E].rearrange("p (k e) -> p k e", e=E), ACT.Copy).then_inc(kept.sem, 1)

            def a1(b):
                xq_turn(act, b)
                pr_full.before(act, b)
                act.activation(xq_t[:, :, :].rearrange("p k (t n) -> p t k n", t=T),
                               bankb(0).rearrange("p (t k n) -> p t k n", t=T, k=KT), ACT.Copy).then_inc(xq_here.sem, 1)

            def a1_q(b):
                qt_turn(act, b)
                act.activation(q_t[:, :, :], bank(1).rearrange("p (k n) -> p k n", k=KT), ACT.Copy).then_inc(qt_here.sem, 1)

            def a1_v(b):
                vt_turn(act, b)
                for t in range(T):
                    act.activation(v8t[t].rearrange("p (c a) d -> p a c d", a=HT),
                                   ps[:, 0:4, t * P:(t + 1) * P].rearrange("p a (c d) -> p a c d", c=4), ACT.Copy).then_inc(vt_here.sem, 1)

            def a2(b):
                for t in range(T):
                    m_turn(act, b, t + 1)
                    act.activation(maxt_a[0:3 * GRP, :], bankb(3)[0:3 * GRP, 0:P], ACT.Copy).then_inc(m_here.sem, 1)
                    for f in range(KT):
                        st_full(act, b, 4 * t + f + 1)
                        if f == 0 and t == 1:
                            oa_full(act, b, 1)
                        act.activation(p_a[:, f * HT:(f + 1) * HT, :], bank(f).rearrange("p (h n) -> p h n", h=HT),
                                       ACT.Exp, scale=DA ** -0.5).then_inc(pa_here.sem, 1)

            def a3_sq(b):
                for t in range(T):
                    outa_here(act, b, t + 1)
                    act.activation(nat[:, t, 0, :], out_a[:, t, :], ACT.Square,
                                   accum_out=st_a[:, 3, t:t + 1]).then_inc(sq_here.sem, 1)

            def a3_t(b):
                oq_turn(act, b)
                act.activation(xq_t[:, :, :].rearrange("p k (t n) -> p t k n", t=T),
                               bankb(0).rearrange("p (t k n) -> p t k n", t=T, k=KT), ACT.Copy).then_inc(oq_here.sem, 1)

            def b1_x1(b):
                for t in range(T):
                    x1_turn(act, b, t + 1)
                    act.activation(x1_t[:, :, t * P:(t + 1) * P], bank(6 + t).rearrange("p (k n) -> p k n", k=KT),
                                   ACT.Copy).then_inc(x1t_here.sem, 1)

            def b1_c(b):
                for t in range(T):
                    c_turn(act, b, t + 1)
                    act.activation(c_t[:, :, t * P:(t + 1) * P], bank(4 + t).rearrange("p (k n) -> p k n", k=KT),
                                   ACT.Copy).then_inc(ct_here.sem, 1)

            def b1_k(b, t):
                q_full(act, b, 2 * t + 1)
                if t:
                    qb_turn(act, b, 2)
                else:
                    qb_turn.before(act, b)
                act.activation(kn[:, :, :, 0:DB], bank(4)[:, 0:2 * P].rearrange("p (s g d) -> p s g d", s=2, g=KVB),
                               ACT.Copy).then_inc(q_first.sem, 1)

            def b1_q(b, t):
                q_full(act, b, 2 * t + 2)
                if t:
                    qb_turn(act, b, 6)
                act.activation(qn[:, :, 0:DB], bank(5).rearrange("p (h d) -> p h d", d=DB),
                               ACT.Copy).then_inc(q_first.sem, 1)

            def b1_keep(b, t):
                for n in range(4):
                    qb_turn(act, b, 6 * t + 2 + n + 1)
                    act.activation(qt_b[:, 4 * t:4 * t + 4, 2 * n:2 * n + 2, :].rearrange("p i g q -> p g i q"),
                                   bankb(6 + n % 2).rearrange("p (g i q) -> p g i q", g=2, i=4),
                                   ACT.Copy).then_inc(qb_act.sem, 1)

            def b2(b):
                mb_turn(act, b)
                act.activation(maxt_b[:, :, :], bankb(4)[0:3 * S, 0:2 * P].rearrange("p (a q) -> p a q", a=2),
                               ACT.Copy).then_inc(mb_here.sem, 1)

            def b3(b, m):
                r, j = m // KB, m % KB
                if m >= 2:
                    pv_done(act, b, m - 1)
                cols = 4 * P if j < KB - 1 else 2 * P
                for s in range(4):
                    n = 4 * m + s
                    stb_full(act, b, n + 1)
                    act.activation(p_b[:, j % 2, s, 0:cols], bank(4 + n % 2)[:, 0:cols], ACT.Exp,
                                   scale=DB ** -0.5).then_inc(pb_here.sem, 1)

            def b3_keep(b, r):
                pv_done(act, b, KB * r + KB)
                if r:
                    ob_turn(act, b, 1)
                act.activation(o_tb[:, :, :], ps[:, 6:8, :].rearrange("p b (i n) -> p (b i) n", i=4),
                               ACT.Copy).then_inc(ob_here.sem, 1)

            def b4(b):
                of_turn(act, b)
                act.activation(o_fb[:, :, :].rearrange("p h (i q) -> p i h q", q=S),
                               ps[:, 6:8, :].rearrange("p b (i h q) -> p (b i) h q", h=G, q=S), ACT.Copy).then_inc(of_here.sem, 1)

            def c1_x2(b):
                for t in range(T):
                    x2_turn(act, b, t + 1)
                    act.activation(x2_t[:, :, t * P:(t + 1) * P], bank(6 + t).rearrange("p (k n) -> p k n", k=KT),
                                   ACT.Copy).then_inc(x2t_here.sem, 1)

            def c1(b):
                lg_here(act, b)
                act.activation(g_c[:, 2, :, :], g_c[:, 1, :, :], ACT.Exp).then_inc(ex_here.sem, 1)

            def c2(b):
                gm_turn(act, b)
                act.activation(gm_t[:, :, :], bank(0)[:, 0:2 * P].rearrange("p (t n) -> p t n", t=T), ACT.Copy).then_inc(gmt_here.sem, 1)

            of = lambda f, n: lambda b: f(b, n)
            run(act, [(A, a1), (C_, c1_x2), (B, b1_c), (B, b1_x1), (C_, c1), (A, a1_q), (B, of(b1_k, 0)), (B, of(b1_q, 0)),
                      (A, a1_v), (B, of(b1_k, 1)), (B, of(b1_keep, 0)), (B, of(b1_q, 1)), (B, of(b1_keep, 1)),
                      (A, a2), (A, a3_sq), (B, b2), (C_, c2), (B, of(b3, 0)), (B, of(b3, 1)), (A, a3_t), (B, of(b3, 2)),
                      (B, of(b3, 3)), (B, of(b3, 4)), (B, of(b3_keep, 0)), (B, of(b3, 5)), (B, of(b3, 6)), (B, of(b3, 7)),
                      (B, of(b3_keep, 1)), (B, b4)])

        @block.tensor
        def _(pe):
            pe.wait_ge(const_in.sem, 32)
            for n in range(4):
                pe.wait_ge(signed.sem, n + 1)
                for k in range(KT):
                    for j in range(4):
                        mm = pe.transpose(bankb(2 * n + k // 2)[:, (k % 2) * C + j * P:(k % 2) * C + (j + 1) * P],
                                          sgn[n % 2][:, j, k * P:(k + 1) * P], eyeb)
                mm.then_inc(turned.sem, 1)
            pe.wait_ge(raw_in[0].sem, 48)
            pe.wait_ge(rout_in.sem, 16)
            pe.wait_ge(kept.sem, 3)
            for k in range(KT):
                for j in range(4):
                    pe.transpose(bank(k)[:, j * P:(j + 1) * P], raw[0][:, j, k * P:(k + 1) * P], eye)
            for k in range(KT):
                mm = pe.transpose(bank(4)[:, k * E:(k + 1) * E], router_nat[0:E, k * P:(k + 1) * P], eye[0:E, 0:E])
            mm.then_inc(turned.sem, 1)
            pe.wait_ge(summed.sem, 4)
            pe.matmul(bank(5)[:, 0:4], ones, abs_sums[:, :], start=True, stop=True).then_inc(total.sem, 1)
            pe.wait_ge(kept.sem, 6)
            pe.wait_ge(scaled.sem, 5)
            pe.wait_ge(w_in.sem, W_IN)
            pe.wait_ge(zeroed.sem, 3)

            def a1(b):
                x_round(pe, b)
                for t in range(T):
                    for k in range(KT):
                        mm = pe.transpose(bankb(0)[:, t * C + k * P:t * C + (k + 1) * P], xq[:, t, k * P:(k + 1) * P], eyeb)
                mm.then_inc(xq_turn.sem, 1)

            def a1_qkv(b, t):
                if t == 0:
                    xq_here(pe, b)
                    za_here.before(pe, b)
                for w in range(3):
                    if t:
                        nat_here(pe, b, w + 1)
                    for k in range(KT):
                        mm = pe.matmul(bank(1 + w), xq_t[:, k, t * P:(t + 1) * P], qkv_sign[:, k, w * C:(w + 1) * C],
                                       start=(k == 0), stop=(k == KT - 1))
                    mm.then_inc(qkv_full.sem, 1)

            def a1_state(b):
                nat_here(pe, b, 4)
                for k in range(KT):
                    mm = pe.transpose(bank(1)[:, k * P:(k + 1) * P], nat[:, 1, 0, k * P:(k + 1) * P], eye)
                mm.then_inc(qt_turn.sem, 1)
                nat_here(pe, b, 5)
                for k in range(KT):
                    mm = pe.matmul(bank(2)[:, k * P:(k + 1) * P], nat[:, 0, 1, k * P:(k + 1) * P], nat[:, 0, 2, k * P:(k + 1) * P],
                                   start=True, stop=True)
                mm.then_inc(kv_full.sem, 1)

            def a1_v(b, t):
                if t == 0:
                    qt_here(pe, b)
                    kv_here(pe, b)
                    if not (isinstance(b, int) and b < 2):
                        gm_here(pe, b - 2)
                t8_here(pe, b, 3 * t + 3)
                carried(pe, "pe")
                for j in range(GRP):
                    c, a = j // HT, j % HT
                    mm = pe.transpose(bank(a)[:, (t * 4 + c) * DA:(t * 4 + c + 1) * DA],
                                      v8[a * S:(a + 1) * S, c * TOK:(c + 1) * TOK, :].rearrange("p n h -> p (n h)"),
                                      eye[a * S:(a + 1) * S, a * S:(a + 1) * S])
                mm.then_inc(vt_turn.sem, 1)

            def a2_s(b, t):
                    bd_here(pe, b, t + 1)
                    t8_here(pe, b)
                    if t == 0:
                        vt_here(pe, b)
                    else:
                        outa_here(pe, b, 1)
                    for c in range(4):
                        pe.matmul(bank(c), tokhot, other, start=True, stop=False)
                        for a in range(HT):
                            mm = pe.matmul(bank(c)[:, a * P:(a + 1) * P], q_bd[:, c, a, :],
                                           k8[:, t, c * TOK:(c + 1) * TOK, :].rearrange("p n h -> p (n h)"),
                                           start=False, stop=(a == HT - 1))
                    mm.then_inc(s_full.sem, 1)

            def a2_x(b, t):
                    m_parts(pe, b, t + 1)
                    carried(pe, "pe")
                    pe.transpose(bankb(3)[0:3 * GRP, 0:P], maxp_a[:, :, :].rearrange("p a h -> p (a h)"), eyeb).then_inc(m_turn.sem, 1)
                    m_here(pe, b, t + 1)
                    for c in range(4):
                        for a in range(HT):
                            pe.matmul(bank(c)[:, a * P:(a + 1) * P], sel[0:3 * GRP + TOK, c * HT + a, :], maxt_a[0:3 * GRP + TOK, :],
                                      start=(a == 0), stop=False)
                        pe.matmul(bank(c), k8[:, t, c * TOK:(c + 1) * TOK, :].rearrange("p n h -> p (n h)"),
                                  q_bd[:, c, :, :].rearrange("p a n -> p (a n)"), start=False, stop=True).then_inc(st_full.sem, 1)

            def a2_v(b, t):
                    for c in range(4):
                        pa_here(pe, b, 4 * t + max(c + 1, 2))
                        for a in range(HT):
                            pe.matmul(bank(0)[a * S:(a + 1) * S, c * P:(c + 1) * P], v8t[t][:, c * HT + a, :],
                                      p_a[:, c * HT + a, :], start=True, stop=True)
                        for a in range(HT):
                            mm = pe.matmul(bank(1)[a * S:(a + 1) * S, c * P:(c + 1) * P], ones[:, 0:S], p_a[:, c * HT + a, :],
                                           start=True, stop=True)
                    mm.then_inc(oa_full.sem, 1)
                    if t == 1:
                        for f in range(KT):
                            mm = pe.matmul(bank(2)[:, f * P:(f + 1) * P], q_t[:, f, :], kv_bd[:, f, :], start=True, stop=True)
                        mm.then_inc(rec_full.sem, 1)

            def a3_t(b):
                o_round(pe, b)
                for t in range(T):
                    for k in range(KT):
                        mm = pe.transpose(bankb(0)[:, t * C + k * P:t * C + (k + 1) * P], xq[:, t, k * P:(k + 1) * P], eyeb)
                mm.then_inc(oq_turn.sem, 1)

            def a3(b):
                if not (isinstance(b, int) and b < 2):
                    zc_here(pe, b - 2)
                oq_here(pe, b)
                for t in range(T):
                    for k in range(KT):
                        mm = pe.matmul(bank(1 + t), xq_t[:, k, t * P:(t + 1) * P], proj_sign[:, k, :], start=(k == 0), stop=(k == KT - 1))
                    mm.then_inc(pr_full.sem, 1)

            def b1_x1(b):
                x2t_here.before(pe, b)
                for t in range(T):
                    x1_here(pe, b, t + 1)
                    for k in range(KT):
                        mm = pe.transpose(bank(6 + t)[:, k * P:(k + 1) * P], x1[:, t, k * P:(k + 1) * P], eye)
                    mm.then_inc(x1_turn.sem, 1)

            def b1_c(b):
                c_here(pe, b)
                zb_here.before(pe, b)
                for t in range(T):
                    for k in range(KT):
                        mm = pe.transpose(bank(4 + t)[:, k * P:(k + 1) * P], c_in[:, t, k * P:(k + 1) * P], eye)
                    mm.then_inc(c_turn.sem, 1)

            def b1_v(b):
                ct_here(pe, b)
                x1t_here(pe, b)
                for j in range(KB):
                    for k in range(KT):
                        for s in range(4):
                            c, src = s // 2, s % 2
                            src_t = (c_t, x1_t)[src]
                            at = 64 * j + S * c
                            mm = pe.matmul(bank(6)[s * S:(s + 1) * S, j * P:(j + 1) * P], src_t[:, k, at:at + S], wkv[:, 2 + src, k, :],
                                           start=(k == 0), stop=(k == KT - 1))
                mm.then_inc(v_full.sem, 1)

            def b1_kq(b, t):
                if t:
                    q_read(pe, b, 1)
                for src in range(2):
                    src_t = (c_t, x1_t)[src]
                    for k in range(KT):
                        mm = pe.matmul(bank(4)[:, src * P:(src + 1) * P], src_t[:, k, t * P:(t + 1) * P], wkv[:, src, k, :],
                                       start=(k == 0), stop=(k == KT - 1))
                mm.then_inc(q_full.sem, 1)
                if t:
                    q_read(pe, b, 2)
                for k in range(2 * KT):
                    src_t = (c_t, x1_t)[k // KT]
                    mm = pe.matmul(bank(5), src_t[:, k % KT, t * P:(t + 1) * P], wq[:, k, :], start=(k == 0), stop=(k == 2 * KT - 1))
                mm.then_inc(q_full.sem, 1)

            def b1_kt(b, t):
                q_slots(pe, b, 2 * t + 1)
                if t == 0:
                    v_here(pe, b)
                for half in range(2):
                    if t:
                        qb_act(pe, b, 3 + half)
                    for g in range(4):
                        for src in range(2):
                            o = bankb(6 + half)[:, g * C // 2:(g + 1) * C // 2].rearrange("p (c s k) -> p c s k", s=2, k=S)[:, :, src, :]
                            mm = pe.transpose(o, kn[:, src, 4 * half + g, :], eyeb)
                    mm.then_inc(qb_turn.sem, 1)

            def b1_qt(b, t):
                q_slots(pe, b, 2 * t + 2)
                for q in range(4):
                    if q < 2:
                        kb_dve(pe, b, 2 * t + q + 1)
                    else:
                        qb_act(pe, b, 4 * t + q - 1)
                    for g in range(2):
                        for hh in range(G):
                            o = bankb(6 + q % 2)[:, g * C:(g + 1) * C].rearrange("p (i h q) -> p i h q", i=4, h=G)[:, :, hh, :]
                            mm = pe.transpose(o, qn[:, (2 * q + g) * G + hh, :], eyeb)
                    mm.then_inc(qb_turn.sem, 1)

            def b2(b, i):
                if i == 0:
                    qb_act(pe, b)
                    kb_dve(pe, b)
                c0 = max(i - 2, 0)
                cols = (i - c0 + 1) * 2 * S
                for half in range(2):
                    if i:
                        sb_max(pe, b, 2 * i + half - 1)
                    for g in range(4):
                        o = bank(4 + 2 * half + g // 2)[:, (g % 2) * 256:(g % 2) * 256 + cols]
                        gg = 4 * half + g
                        pe.matmul(o, qt_b[:, i, gg, :], kt_b[:, gg, c0:i + 1, :].rearrange("p c k -> p (c k)"), start=True, stop=False)
                        if i < 2:
                            mm = pe.matmul(o[:, cols - 2 * S:cols], rep, mask_nat[:, 1, :], start=False, stop=True)
                        else:
                            mm = pe.matmul(o.rearrange("p (c k) -> p c k", c=3)[:, 0:3:2, :], rep, mask_nat, start=False, stop=True)
                    mm.then_inc(sb_full.sem, 1)

            def b2_max(b):
                mb_parts(pe, b)
                for a in range(2):
                    mm = pe.transpose(bankb(4)[0:3 * S, a * P:(a + 1) * P], maxp_b[:, a, :, :, :].rearrange("p a i g -> p (a i g)"), eyeb)
                mm.then_inc(mb_turn.sem, 1)

            def b3_s(b, m):
                if m == 0:
                    mb_here(pe, b)
                    mb_sent(pe, b)
                r, j = m // KB, m % KB
                cols = 4 * P if j < KB - 1 else 2 * P
                for s in range(4):
                    g, n = 4 * r + s, 4 * m + s
                    if n >= 2:
                        pb_here(pe, b, n - 1)
                    pe.matmul(bank(4 + n % 2)[:, 0:cols], kt_b[:, g, 2 * j:2 * j + 2, :].rearrange("p c k -> p (c k)"),
                              qt_b[:, 2 * j:2 * j + cols // P, g, :], start=True, stop=False)
                    pe.matmul(bank(4 + n % 2)[:, 0:cols], key, mask_tr[:, 0:cols], start=False, stop=True).then_inc(stb_full.sem, 1)

            def b3_w(b, m):
                r, j = m // KB, m % KB
                pb_here(pe, b, 4 * m + 4)
                if r and j == 0:
                    ob_here(pe, b, 1)
                for half in range(2 if j < KB - 1 else 1):
                    at = 2 * j + 2 * half
                    for s in range(4):
                        mm = pe.matmul(bank(6 + at // 4)[s * S:(s + 1) * S, (at % 4) * P:(at % 4) * P + 2 * P], v_b[:, j, 4 * r + s, :],
                                       p_b[:, j % 2, s, half * 2 * P:(half + 1) * 2 * P],
                                       start=(at == 0 or (j == 1 and half == 1)), stop=True, skip_group_check=True)
                mm.then_inc(pv_done.sem, 1)

            def b3_back(b):
                for r in range(2):
                    ob_here(pe, b, r + 1)
                    if r:
                        on_here(pe, b, 1)
                    for i in range(QB):
                        mm = pe.transpose(bank(4 + i // 4)[:, (i % 4) * P:(i % 4 + 1) * P], o_tb[:, i, :], eye)
                    mm.then_inc(ob_turn.sem, 1)

            def b4(b):
                on_here(pe, b)
                for i in range(QB):
                    mm = pe.transpose(bank(6 + i // 4)[:, (i % 4) * P:(i % 4 + 1) * P], on_b[:, i, :, :].rearrange("p g d -> p (g d)"), eye)
                mm.then_inc(of_turn.sem, 1)
                of_here(pe, b)
                for t in range(T):
                    for k in range(G):
                        mm = pe.matmul(bank(4 + t), o_fb[:, k, t * P:(t + 1) * P], wo[:, k, :], start=(k == 0), stop=(k == G - 1))
                    mm.then_inc(wo_full.sem, 1)

            def c1_x2(b):
                for t in range(T):
                    x2_here(pe, b, t + 1)
                    for k in range(KT):
                        mm = pe.transpose(bank(6 + t)[:, k * P:(k + 1) * P], x2[:, t, k * P:(k + 1) * P], eye)
                    mm.then_inc(x2_turn.sem, 1)

            def c1(b):
                x2t_here(pe, b)
                for t in range(T):
                    for k in range(KT):
                        mm = pe.matmul(bank(0)[:, t * 256:t * 256 + E + P], x2_t[:, k, t * P:(t + 1) * P], rl[:, k, :], start=(k == 0), stop=(k == KT - 1))
                mm.then_inc(rl_full.sem, 1)

            def c2(b):
                zc_here.before(pe, b)
                if isinstance(b, int) and b + 2 >= NB:
                    za_here(pe, NB - 1)
                else:
                    outa_here(pe, b + 2)
                gm_here(pe, b)
                for t in range(T):
                    mm = pe.transpose(bank(0)[:, t * P:(t + 1) * P], gm[:, t, :], eye)
                mm.then_inc(gm_turn.sem, 1)
                for t in range(T):
                    for k in range(KT):
                        pe.matmul(bank(1 + t), x2_t[:, k, t * P:(t + 1) * P], base_t[:, k, :], start=(k == 0), stop=False)
                    if t == 0:
                        gmt_here(pe, b)
                    pe.matmul(bank(1 + t), gm_t[:, t, :], lora_b[:, :], start=False, stop=True).then_inc(ff_full.sem, 1)

            of = lambda f, n: lambda b: f(b, n)
            run(pe, [(A, a1), (A, of(a1_qkv, 0)), (C_, c1_x2), (B, b1_c), (A, of(a1_qkv, 1)), (B, b1_x1), (C_, c1), (B, b1_v),
                     (A, a1_state), (B, of(b1_kq, 0)), (A, of(a1_v, 0)), (B, of(b1_kt, 0)), (A, of(a1_v, 1)),
                     (B, of(b1_kq, 1)), (B, of(b1_qt, 0)), (B, of(b1_kt, 1)), (A, of(a2_s, 0)), (B, of(b1_qt, 1)),
                     (B, of(b2, 0)), (A, of(a2_x, 0)), (B, of(b2, 1)), (A, of(a2_v, 0)), (B, of(b2, 2)), (B, of(b2, 3)),
                     (A, of(a2_s, 1)), (B, of(b2, 4)), (A, of(a2_x, 1)), (B, of(b2, 5)), (A, of(a2_v, 1)), (B, of(b2, 6)),
                     (B, of(b2, 7)), (B, b2_max), (C_, c2), (B, of(b3_s, 0)), (B, of(b3_s, 1)), (B, of(b3_w, 0)), (A, a3_t),
                     (B, of(b3_s, 2)), (B, of(b3_w, 1)), (A, a3), (B, of(b3_s, 3)), (B, of(b3_w, 2)), (B, of(b3_s, 4)),
                     (B, of(b3_w, 3)), (B, of(b3_s, 5)), (B, of(b3_w, 4)), (B, of(b3_s, 6)), (B, of(b3_w, 5)),
                     (B, of(b3_s, 7)), (B, of(b3_w, 6)), (B, of(b3_w, 7)), (B, b3_back), (B, b4)])

        @block.vector
        def _(dve):
            for n in range(4):
                dve.wait_ge(raw_in[n % 2].sem, 16 * (n // 2 + 1))
                dve.tensor_reduce(abs_sums[:, n:n + 1], raw[n % 2], AX.XY, ALU.add, apply_absolute_value=True).then_inc(summed.sem, 1)
            dve.wait_ge(total.sem, 1)
            links = [0]

            def link0(ins):
                links[0] += 1
                ins.then_inc(scaled.sem, 1)
                dve.wait_ge(scaled.sem, links[0])

            link0(dve.tensor_reduce(wscale[:, 2:3], bank(5)[:, 0:3], AX.X, ALU.add))
            link0(dve.tensor_copy(wscale[:, 3:4], bank(5)[:, 3:4]))
            link0(dve.tensor_scalar(wscale[:, 0:1], wscale[:, 2:3], 1.0 / (3 * C * C), 1e-5, ALU.mult, ALU.max))
            link0(dve.tensor_scalar(wscale[:, 1:2], wscale[:, 3:4], 1.0 / (C * C), 1e-5, ALU.mult, ALU.max))
            link0(dve.tensor_scalar(wscale[:, 0:2], wscale[:, 0:2], 1.0 / 127.0, None, ALU.mult))
            dve.wait_ge(const_in.sem, 32)
            dve.wait_ge(zeroed.sem, 3)
            dve.wait_ge(w_in.sem, W_IN)

            def a0(b):
                c = ch["a1"]; c.start(dve, b)
                x_here(dve, b)
                dve.tensor_reduce(st_a[:, 7, :], x_in[:, :, :], AX.X, ALU.max, apply_absolute_value=True).then_inc(tmpa.sem, 1)
                tmpa(dve, b)
                c.link(dve.tensor_scalar(st_a[:, 0, :], st_a[:, 7, :], 1e-5, None, ALU.max))
                dve.reciprocal(st_a[:, 1, :], st_a[:, 0, :]).then_inc(a_max.sem, 1)
                c.link(dve.tensor_scalar(st_a[:, 2, :], st_a[:, 0, :], wscale[:, 0:1], None, ALU.mult))
                c.end()

            def a0_round(b):
                x_scaled(dve, b)
                oq_turn.before(dve, b)
                dve.tensor_scalar(xq[:, :, :], y_a[:, :, :], MAGIC, MAGIC, ALU.add, ALU.subtract).then_inc(x_round.sem, 1)

            def a1_nat(b, t):
                for w in range(3):
                    qkv_full(dve, b, 3 * t + w + 1)
                    dve.scalar_tensor_tensor(nat[:, t, w, :], bank(1 + w), st_a[:, 2, t:t + 1], qkv_bias[:, w * C:(w + 1) * C],
                                             ALU.mult, ALU.add).then_inc(nat_here.sem, 1)

            def a1_t8(b, t, which):
                for w in which:
                    dst = (q8[:, t, :, :], k8[:, t, :, :], v8[:, :, :])[w]
                    nat_here(dve, b, 3 * t + w + 1)
                    if t and w == 2:
                        vt_turn(dve, b, 1)
                    dve.transpose(dst.rearrange("p n h -> p h n"), nat[:, t, w, :].rearrange("p (h d) -> p h d", d=DA)).then_inc(t8_here.sem, 1)

            def a1_state(b):
                kv_full(dve, b)
                for s in range(HT):
                    ins = dve.tensor_copy(kv_bd[s * S:(s + 1) * S, :, s * S:(s + 1) * S],
                                          bank(2)[s * S:(s + 1) * S, :].rearrange("p (k n) -> p k n", k=KT)[:, :, s * S:(s + 1) * S])
                ins.then_inc(kv_here.sem, 1)

            def a2_max(b, t):
                    c = ch["a2"]
                    if t == 0:
                        c.start(dve, b)
                    s_full(dve, b, t + 1)
                    dve.tensor_reduce(max_a[:, 0, :], ps[:, 0:4, :].rearrange("p b (h n) -> p (b h) n", h=HT), AX.X, ALU.max).then_inc(s_max.sem, 1)
                    s_max(dve, b, t + 1)
                    c.link(dve.tensor_scalar(maxp_a[:, 0, :], max_a[:, 0, :], -1.0, None, ALU.mult))
                    c.link(dve.scalar_tensor_tensor(max_a[:, 1, :], max_a[:, 0, :], -1.0, maxp_a[:, 0, :], ALU.mult, ALU.subtract))
                    c.link(dve.tensor_copy(maxp_a[:, 1, :], max_a[:, 1, :]))
                    dve.tensor_tensor(maxp_a[:, 2, :], max_a[:, 1, :], maxp_a[:, 1, :], ALU.subtract).then_inc(m_parts.sem, 1)

            def a2_out(b, t):
                    c = ch["a2"]
                    bd_here(dve, b)
                    oa_full(dve, b, t + 1)
                    back = lambda k: bank(k).rearrange("p (n h) -> p h n", h=HA)
                    c.link(dve.transpose(sum_a[:, :, :], back(1)))
                    c.link(dve.transpose(out_a[:, t, :].rearrange("p (h d) -> p h d", d=DA), back(0)))
                    c.link(dve.reciprocal(rinv_a[:, :], sum_a[:, :, 0]))
                    ins = dve.tensor_tensor(out_a[:, t, :].rearrange("p (h d) -> p h d", d=DA),
                                            out_a[:, t, :].rearrange("p (h d) -> p h d", d=DA),
                                            rinv_a[:, :].unsqueeze(2).to_broadcast([P, HA, DA]), ALU.mult)
                    if t == 0:
                        ins.then_inc(outa_here.sem, 1)
                    else:
                        ins.then_inc(out1.sem, 1)
                        out1(dve, b)
                        rec_full(dve, b)
                        dve.tensor_tensor(out_a[:, t, :], bank(2), out_a[:, t, :], ALU.add).then_inc(outa_here.sem, 1)
                        c.end()

            def a3(b):
                c = ch["a3"]; c.start(dve, b)
                sq_here(dve, b)
                dve.tensor_scalar(rs_a[:, 0, :], st_a[:, 3, :], 1.0 / C, EPS_RMS, ALU.mult, ALU.add).then_inc(ms_here.sem, 1)
                rms_here(dve, b)
                for t in range(T):
                    ins = dve.scalar_tensor_tensor(out_a[:, t, :], out_a[:, t, :], rs_a[:, 1, t:t + 1], norm_w[:, :], ALU.mult, ALU.mult)
                c.link(ins)
                c.link(dve.tensor_reduce(st_a[:, 7, :], out_a[:, :, :], AX.X, ALU.max, apply_absolute_value=True))
                c.link(dve.tensor_scalar(st_a[:, 4, :], st_a[:, 7, :], 1e-5, None, ALU.max))
                dve.reciprocal(st_a[:, 5, :], st_a[:, 4, :]).then_inc(b_max.sem, 1)
                c.link(dve.tensor_scalar(st_a[:, 6, :], st_a[:, 4, :], wscale[:, 1:2], None, ALU.mult))
                c.end()
                o_scaled(dve, b)
                xq_turn(dve, b)
                dve.tensor_scalar(xq[:, :, :], y_a[:, :, :], MAGIC, MAGIC, ALU.add, ALU.subtract).then_inc(o_round.sem, 1)

            def a3_z(b):
                x_kept(dve, b)
                for t in range(T):
                    pr_full(dve, b, t + 1)
                    dve.scalar_tensor_tensor(out_a[:, t, :], bank(1 + t), st_a[:, 6, t:t + 1], x_res[:, t, :], ALU.mult, ALU.add).then_inc(za_here.sem, 1)

            def norm_stats(c, z, mv, rs, row, here):
                for t in range(T):
                    c.link(dve.bn_stats(stats[:, t, :], z[:, t, :]))
                carried(dve, "dve")
                for t in range(T):
                    ins = dve.bn_aggr(mv[:, t, :], stats[:, t, :])
                c.link(ins)
                dve.tensor_scalar(rs[:, row, :], mv[:, :, 1], EPS_LN, None, ALU.add).then_inc(here.sem, 1)

            def norm_apply(b, z, mv, rs, row, rstd, dst, done):
                rstd(dve, b)
                for t in range(T):
                    ins = dve.tensor_scalar(dst[:, t, :], z[:, t, :], mv[:, t, 0:1], rs[:, row + 1, t:t + 1], ALU.subtract, ALU.mult)
                    if done.per == T or t == T - 1:
                        ins.then_inc(done.sem, 1)

            def a4_stats(b):
                c = ch["a4"]; c.start(dve, b)
                za_here(dve, b)
                norm_stats(c, out_a, mv_a, rs_a, 2, va_here)
                c.end()

            def a4(b):
                x2_here.before(dve, b)
                norm_apply(b, out_a, mv_a, rs_a, 2, ra_here, x1, x1_here)

            def b1_v(b):
                v_full(dve, b)
                dve.tensor_copy(v_b[:, :, :, 0:DB], bank(6).rearrange("p (j g d) -> p j g d", j=KB, g=KVB)).then_inc(v_here.sem, 1)

            def b1_k(b, t):
                c = ch["b1"]
                if t == 0:
                    c.start(dve, b)
                q_first(dve, b, 2 * t + 1)
                k1 = kn[:, :, :, :].rearrange("p s g c -> p (s g) c")
                kr = k_rest[:, :].rearrange("p (h d) -> p h d", d=DB)
                dve.tensor_copy(k1[:, :, 96:128], kx[:, t:t + 1, :].to_broadcast([P, 2 * KVB, S]))
                dve.tensor_tensor(kr, bank(4)[:, 0:2 * P].rearrange("p (h d) -> p h d", d=DB), k1[:, :, 0:DB], ALU.subtract).then_inc(q_read.sem, 1)
                q_read(dve, b, 2 * t + 1)
                dve.tensor_copy(k1[:, :, 3 * DB:4 * DB], k1[:, :, 0:DB])
                dve.tensor_copy(k1[:, :, 5 * DB:6 * DB], k1[:, :, 0:DB])
                dve.tensor_copy(k1[:, :, 4 * DB:5 * DB], kr)
                c.link(dve.tensor_copy(k1[:, :, DB:2 * DB], kr))
                dve.tensor_tensor(k1[:, :, 2 * DB:3 * DB], kr, k1[:, :, DB:2 * DB], ALU.subtract).then_inc(q_slots.sem, 1)

            def b1_q(b, t):
                c = ch["b1"]
                q_first(dve, b, 2 * t + 2)
                qr = q_rest[:, :].rearrange("p (h d) -> p h d", d=DB)
                dve.tensor_tensor(qr, bank(5).rearrange("p (h d) -> p h d", d=DB), qn[:, :, 0:DB], ALU.subtract).then_inc(q_read.sem, 1)
                q_read(dve, b, 2 * t + 2)
                dve.tensor_copy(qn[:, :, 96:128], qx)
                dve.tensor_copy(qn[:, :, DB:2 * DB], qn[:, :, 0:DB])
                dve.tensor_copy(qn[:, :, 2 * DB:3 * DB], qn[:, :, 0:DB])
                dve.tensor_copy(qn[:, :, 4 * DB:5 * DB], qr)
                c.link(dve.tensor_copy(qn[:, :, 3 * DB:4 * DB], qr))
                dve.tensor_tensor(qn[:, :, 5 * DB:6 * DB], qr, qn[:, :, 3 * DB:4 * DB], ALU.subtract).then_inc(q_slots.sem, 1)
                if t == T - 1:
                    c.end()

            def b1_keep(b, t):
                for n in range(2):
                    qb_turn(dve, b, 6 * t + n + 1)
                    dve.tensor_copy(kt_b[:, 4 * n:4 * n + 4, 4 * t:4 * t + 4, :],
                                    bankb(6 + n).rearrange("p (g c k) -> p g c k", g=4, c=4)).then_inc(kb_dve.sem, 1)

            def b2(b, i):
                cols = (min(i, 2) + 1) * 2 * S
                for half in range(2):
                    sb_full(dve, b, 2 * i + half + 1)
                    dve.tensor_reduce(max_b[:, 0, i, 4 * half:4 * half + 4],
                                      ps[:, 4 + 2 * half:6 + 2 * half, :].rearrange("p b (g n) -> p (b g) n", g=2)[:, :, 0:cols],
                                      AX.X, ALU.max).then_inc(sb_max.sem, 1)

            def b2_max(b):
                c = ch["b2"]; c.start(dve, b)
                sb_max(dve, b)
                m0 = max_b[:, 0, :, :].rearrange("p (a i) g -> p a i g", a=2)
                m1 = max_b[:, 1, :, :].rearrange("p (a i) g -> p a i g", a=2)
                for a in range(2):
                    ins = dve.tensor_scalar(maxp_b[:, a, 0, :, :], m0[:, a], -1.0, None, ALU.mult)
                c.link(ins)
                for a in range(2):
                    ins = dve.scalar_tensor_tensor(m1[:, a], m0[:, a], -1.0, maxp_b[:, a, 0, :, :], ALU.mult, ALU.subtract)
                c.link(ins)
                for a in range(2):
                    ins = dve.tensor_copy(maxp_b[:, a, 1, :, :], m1[:, a])
                c.link(ins)
                for a in range(2):
                    ins = dve.tensor_tensor(maxp_b[:, a, 2, :, :], m1[:, a], maxp_b[:, a, 1, :, :], ALU.subtract)
                ins.then_inc(mb_parts.sem, 1)
                c.end()

            def b3(b):
                c = ch["b3"]; c.start(dve, b)
                for r in range(2):
                    ob_turn(dve, b, r + 1)
                    o = ps[:, 4:6, :].rearrange("p b (i s c) -> p (b i) s c", i=4, s=4)
                    c.link(dve.reciprocal(rinv_b[:, :, :], o[:, :, :, DB]))
                    dve.tensor_tensor(on_b[:, :, 4 * r:4 * r + 4, :], o[:, :, :, 0:DB],
                                      rinv_b[:, :, :].unsqueeze(3).to_broadcast([P, QB, 4, DB]), ALU.mult).then_inc(on_here.sem, 1)
                c.end()

            def b4(b):
                c = ch["b4"]; c.start(dve, b)
                for t in range(T):
                    wo_full(dve, b, t + 1)
                    dve.tensor_tensor(x1[:, t, :], bank(4 + t), x1[:, t, :], ALU.add).then_inc(zb_here.sem, 1)
                zb_here(dve, b)
                y_sent.before(dve, b)
                norm_stats(c, x1, mv_b, rs_b, 0, vb_here)
                c.end()
                norm_apply(b, x1, mv_b, rs_b, 0, rb_here, x2, x2_here)

            def c1(b):
                c = ch["c1"]; c.start(dve, b)
                rl_full(dve, b)
                wide = lambda r: gs_c[:, r, :].unsqueeze(2).to_broadcast([P, T, E])
                gr = lambda k: g_c[:, k, :, :]
                rmp = ramp.unsqueeze(1).to_broadcast([P, T, E])
                pl = bank(0).rearrange("p (t n) -> p t n", t=T)
                c.link(dve.tensor_tensor(gr(0), pl[:, :, 0:E], router_bias[:, :].unsqueeze(1).to_broadcast([P, T, E]), ALU.add))
                c.link(dve.tensor_reduce(gs_c[:, 0, :], gr(0), AX.X, ALU.max))
                dve.tensor_tensor(gr(1), gr(0), wide(0), ALU.subtract).then_inc(lg_here.sem, 1)
                ex_here(dve, b)
                at = 2
                for n in range(2):
                    c.link(dve.tensor_reduce(gs_c[:, 1 + n, :], gr(at), AX.X, ALU.max))
                    c.link(dve.tensor_tensor(gr(3), gr(at), wide(1 + n), ALU.is_equal))
                    c.link(dve.tensor_tensor(gr(4), gr(3), rmp, ALU.mult))
                    c.link(dve.tensor_reduce(gs_c[:, 3, :], gr(4), AX.X, ALU.max))
                    c.link(dve.tensor_tensor(gr(6 + n), gr(4), wide(3), ALU.is_equal))
                    if n == 0:
                        c.link(dve.scalar_tensor_tensor(gr(5), gr(6), -2.0, gr(2), ALU.mult, ALU.add))
                        at = 5
                c.link(dve.tensor_tensor(gr(8), gr(6), gr(7), ALU.add))
                c.link(dve.tensor_tensor(gr(9), gr(8), gr(2), ALU.mult))
                ins = dve.tensor_reduce(gs_c[:, 4, :], gr(9), AX.X, ALU.add)
                ins.then_inc(g1.sem, 1); g1(dve, b, 1)
                dve.reciprocal(gs_c[:, 5, :], gs_c[:, 4, :]).then_inc(g1.sem, 1); g1(dve, b, 2)
                dve.scalar_tensor_tensor(gr(10), gr(9), SCALING, wide(5), ALU.mult, ALU.mult).then_inc(g1.sem, 1); g1(dve, b, 3)
                gm_turn.before(dve, b)
                for t in range(T):
                    ins = dve.tensor_tensor(gm[:, t, :].rearrange("p (e r) -> p e r", e=E), pl[:, t, E:E + P].rearrange("p (e r) -> p e r", e=E),
                                            g_c[:, 10, t, :].unsqueeze(2).to_broadcast([P, E, R]), ALU.mult)
                ins.then_inc(gm_here.sem, 1)
                c.end()

            def c2(b):
                c = ch["c2"]; c.start(dve, b)
                x2_kept(dve, b)
                for t in range(T):
                    ff_full(dve, b, t + 1)
                    dve.tensor_tensor(z_c[:, t, :], bank(1 + t), z_c[:, t, :], ALU.add).then_inc(zc_here.sem, 1)
                zc_here(dve, b)
                norm_stats(c, z_c, mv_c, rs_c, 0, vc_here)
                c.end()
                norm_apply(b, z_c, mv_c, rs_c, 0, rc_here, z_c, y_here)

            of = lambda f, *n: lambda b: f(b, *n)
            run(dve, [(A, of(a1_nat, 0)), (A, of(a1_t8, 0, (0, 1, 2))), (A, of(a1_nat, 1)), (A, of(a1_t8, 1, (0, 1))), (C_, c1),
                      (B, b1_v), (A, a1_state), (B, of(b1_k, 0)), (A, of(a1_t8, 1, (2,))), (B, of(b1_q, 0)), (B, of(b1_keep, 0)),
                      (B, of(b1_k, 1)), (B, of(b1_q, 1)), (B, of(b1_keep, 1)),
                      (A, of(a2_max, 0)), (B, of(b2, 0)), (B, of(b2, 1)), (B, of(b2, 2)), (A, of(a2_out, 0)), (B, of(b2, 3)),
                      (A, of(a2_max, 1)), (B, of(b2, 4)), (B, of(b2, 5)), (B, of(b2, 6)), (A, of(a2_out, 1)), (B, of(b2, 7)),
                      (B, b2_max), (A, a3), (C_, c2), (A, a3_z), (A, a4_stats), (NEXT, a0), (NEXT, a0_round), (B, b3), (B, b4), (A, a4)])


_INS = ["x", "ctx_2048", "L0_attn_qkv_w", "L0_attn_qkv_b", "L0_attn_proj_w", "L0_attn_proj_b", "L0_attn_norm_w",
        "L0_xattn_Wq", "L0_xattn_Wk", "L0_xattn_Wv", "L0_xattn_Wsk", "L0_xattn_Wsv", "L0_xattn_Wo",
        "L0_ffn_base_w", "L0_ffn_base_b", "L0_ffn_router_w", "L0_ffn_router_b", "L0_ffn_lora_A", "L0_ffn_lora_B"]


def kernel(**inputs):
    import ml_dtypes
    import concourse.bacc as bacc
    from concourse.bass_utils import run_bass_kernel_spmd

    nc = bacc.Bacc("TRN2", target_bir_lowering=False, num_devices=1)
    (_, f_arr), (_, b_arr) = constants()
    arrays = {name: np.ascontiguousarray(inputs[name]) for name in _INS}
    arrays["const_f"] = f_arr
    arrays["const_b"] = b_arr.astype(ml_dtypes.bfloat16)
    d = {name: nc.dram_tensor(name, a.shape, mybir.dt.from_np(a.dtype), kind="ExternalInput").ap()
         for name, a in arrays.items()}
    out = nc.dram_tensor("y", (NB, N, C), F32, kind="ExternalOutput").ap()
    program(nc, d, out)
    r = run_bass_kernel_spmd(nc, [arrays], core_ids=[0])
    return r.results[0]["y"]
```

```python
from contextlib import ExitStack

import numpy as np

import concourse.bass as bass
from concourse import mybir

F32 = mybir.dt.float32
BF16 = mybir.dt.bfloat16
ALU = mybir.AluOpType
ACT = mybir.ActivationFunctionType
AX = mybir.AxisListType

P = 128
S = 32
NB, N, C = 8, 256, 512
T = N // P
KT = C // P
HA, DA = 16, 32
HT = P // DA
TOK = P // HA
GRP = P // TOK
HB, KVB, DB = 32, 8, 16
G = HB // KVB
WIN = 64
QB = N // S
KB = N // (2 * S)
E, R = 8, 16
SCALING = 2.0
EARLY, LATE = 6, 4 + 2 + KVB + KT
BIG = -1.0e30
MAGIC = 12582912.0
EPS_RMS, EPS_LN = 1e-6, 1e-5


def constants():
    f = {}
    f["eye"] = np.eye(P)
    f["ones"] = np.ones((P, P))
    f["ramp"] = np.broadcast_to(np.arange(E, 0, -1.0), (P, E))
    f["strip"] = np.repeat(np.eye(HT), S, axis=0)
    f["neghalf"] = np.full((P, 2), -0.5)
    b = {}
    b["eye"] = np.eye(P)
    tok = np.arange(P) // HA
    sel = np.zeros((P, GRP, P))
    for p in range(3):
        for j in range(GRP):
            sel[p * GRP + j, j, :] = 1
    for r in range(TOK):
        sel[3 * GRP + r, :, :] = tok == r
    b["sel"] = sel.reshape(P, -1)
    low = np.zeros((P, P))
    for r in range(TOK):
        low[3 * GRP + r] = np.where(tok == r, 0.0, BIG)
    b["maxt0"] = low
    tokhot, other = np.zeros((P, P)), np.zeros((P, 4, P))
    for r in range(TOK):
        tokhot[r] = tok == r
        other[r] = np.where(tok == r, 0.0, BIG)
    b["tokhot"], b["other"] = tokhot, other.reshape(P, -1)
    rep = np.zeros((P, P))
    for q in range(S):
        rep[q, q::S] = 1
    b["rep"] = rep
    q, k = np.arange(S)[:, None], np.arange(S)[None, :]
    m = np.zeros((P, 2, 2, S))
    m[:S, 0] = np.where(k > q, 0.0, BIG)[:, None]
    m[:S, 1] = np.where(k <= q, 0.0, BIG)[:, None]
    b["mask_nat"] = m.reshape(P, -1)
    key = np.zeros((P, 2, 2, S))
    for r in range(2 * S):
        key[r, r // S, :, r % S] = 1
    b["key"] = key.reshape(P, -1)
    r = np.arange(2 * S)[:, None, None, None]
    qq = (np.arange(4)[:, None, None] * S + np.arange(S)[None, None, :])[None]
    ok = np.broadcast_to((qq - r >= 0) & (qq - r < WIN), (2 * S, 4, G, S))
    m = np.zeros((P, 4 * P))
    m[:2 * S] = np.where(ok, 0.0, BIG).reshape(2 * S, -1)
    b["mask_tr"] = m
    slope = (np.power(np.float32(2.0), (-8.0 * np.arange(HB, dtype=np.float32) / HB)) * np.float32(DB ** 0.5)).astype(np.float32)
    trunc = lambda v: (v.astype(np.float32).view(np.uint32) & 0xFFFF0000).view(np.float32)
    s1 = trunc(slope); s2 = trunc(slope - s1); s3 = slope - s1 - s2
    qx = np.zeros((HB, S)); qx[:, 3], qx[:, 4], qx[:, 5] = s1, s2, s3
    b["qx"] = np.broadcast_to(qx[None], (P, HB, S)).reshape(P, -1)
    kx = np.zeros((P, T, S)); kx[:, :, 0:3] = 1
    for t in range(T):
        kx[:, t, 3:6] = (np.arange(P) + P * t - N // 2)[:, None]
    b["kx"] = kx.reshape(P, -1)
    def pack(d):
        at, cols = {}, 0
        for name, a in d.items():
            at[name] = (cols, a.shape[1]); cols += a.shape[1]
        return at, np.concatenate(list(d.values()), axis=1).astype(np.float32)
    return pack(f), pack(b)


def program(nc, d, out):
    (f_at, f_arr), (b_at, b_arr) = constants()
    ctx = ExitStack()
    with ctx:
        def sb(name, shape, dt=F32):
            return ctx.enter_context(nc.sbuf_tensor(name, shape, dt))

        class Signal:

            def __init__(self, name, per):
                self.sem = ctx.enter_context(nc.semaphore(name))
                self.per = per

            def upto(self, b, k=None):
                return self.per * b + (self.per if k is None else k)

            def __call__(self, eng, b, k=None):
                eng.wait_ge(self.sem, self.upto(b, k))

            def before(self, eng, b):
                if not (isinstance(b, int) and b == 0):
                    eng.wait_ge(self.sem, self.per * b)

        class Chain:

            def __init__(self, name, per):
                self.s = Signal(name, per)
                self.k = 0

            def start(self, eng, b):
                self.eng, self.b, self.k = eng, b, 0

            def link(self, ins):
                self.k += 1
                ins.then_inc(self.s.sem, 1)
                self.eng.wait_ge(self.s.sem, self.s.per * self.b + self.k)

            def end(self):
                assert self.k == self.s.per, (self.k, self.s.per)

        cf = sb("cf", [P, f_arr.shape[1]])
        cb = sb("cb", [P, b_arr.shape[1]], BF16)
        fc = lambda n: cf[:, f_at[n][0]:f_at[n][0] + f_at[n][1]]
        bc = lambda n: cb[:, b_at[n][0]:b_at[n][0] + b_at[n][1]]
        eye, ones, ramp, strip, neghalf = fc("eye"), fc("ones"), fc("ramp"), fc("strip"), fc("neghalf")
        eyeb, rep, key, mask_tr = bc("eye"), bc("rep"), bc("key"), bc("mask_tr")
        sel = bc("sel").rearrange("p (h g) -> p h g", h=GRP)
        tokhot, other = bc("tokhot"), bc("other")
        mask_nat = bc("mask_nat").rearrange("p (r k) -> p r k", r=2)
        qx = bc("qx").rearrange("p (h c) -> p h c", h=HB)
        kx = bc("kx").rearrange("p (t c) -> p t c", t=T)

        qkv_sign = sb("qkv_sign", [P, KT, 3 * C], BF16)
        proj_sign = sb("proj_sign", [P, KT, C], BF16)
        base_t = sb("base_t", [P, KT, C])
        wq = sb("wq", [P, 2 * KT, C])
        wkv = sb("wkv", [P, 4, KT, P])
        wo = sb("wo", [P, G, C])
        rl = sb("rl", [P, KT, E + P])
        lora_b = sb("lora_b", [P, C])
        qkv_bias = sb("qkv_bias", [P, 3 * C])
        proj_bias = sb("proj_bias", [P, C])
        norm_w = sb("norm_w", [P, C])
        base_bias = sb("base_bias", [P, C])
        router_bias = sb("router_bias", [P, E])
        abs_sums = sb("abs_sums", [P, 4])
        wscale = sb("wscale", [P, 4])

        x_in = sb("x_in", [P, T, C])
        x_res = sb("x_res", [P, T, C])
        xq = sb("xq", [P, T, C], BF16)
        xq_t = sb("xq_t", [P, KT, N], BF16)
        st_a = sb("st_a", [P, 8, T])
        nat = sb("nat", [P, T, 3, C])
        y_a = nat[:, :, 1, :]
        q_t = sb("q_t", [P, KT, P])
        k8 = sb("k8", [P, T, S, HA])
        q_bd = sb("q_bd", [P, 4, HT, P])
        v8t = [nat[:, t, t, :].rearrange("p (j d) -> p j d", j=GRP) for t in range(T)]
        kv_bd = sb("kv_bd", [P, KT, P])
        p_a = sb("p_a", [P, HA, P])
        max_a = sb("max_a", [P, 3, HA])
        maxp_a = sb("maxp_a", [P, 3, HA], BF16)
        maxt_a = sb("maxt_a", [P, P], BF16)
        sum_a = sb("sum_a", [P, HA, DA])
        v8 = sum_a[:, :, :].rearrange("p a b -> p (a b)").rearrange("p (n h) -> p n h", h=HA)
        rinv_a = sb("rinv_a", [P, HA])
        out_a = sb("out_a", [P, T, C])
        q8 = out_a[:, :, :].rearrange("p t (n h) -> p t n h", h=HA)
        stats = sb("stats", [P, T, 6])
        mv_a = sb("mv_a", [P, T, 2])
        rs_a = sb("rs_a", [P, 4, T])
        x1 = sb("x1", [P, T, C])
        x1_t = sb("x1_t", [P, KT, N])

        c_in = sb("c_in", [P, T, C])
        p_b = sb("p_b", [P, 2, 4, 4 * P])
        flat = p_b[:, :, :, :].rearrange("p a b c -> p (a b c)")
        c_t = flat[:, 0:KT * N].rearrange("p (k n) -> p k n", k=KT)
        kn = flat[:, KT * N:2 * KT * N].bitcast(BF16).rearrange("p (s g c) -> p s g c", s=2, g=KVB)
        qn = flat[:, 2 * KT * N:4 * KT * N].bitcast(BF16).rearrange("p (h c) -> p h c", h=HB)
        q_rest = c_in[:, 0, :]
        k_rest = c_in[:, 1, 0:2 * P]
        qt_b = sb("qt_b", [P, QB, KVB, P], BF16)
        kt_b = sb("kt_b", [P, KVB, QB, 2 * S], BF16)
        v_b = sb("v_b", [P, KB, KVB, S])
        max_b = sb("max_b", [P, 2, QB, KVB])
        maxp_b = sb("maxp_b", [P, 2, 3, QB // 2, KVB], BF16)
        maxt_b = sb("maxt_b", [3 * S, 2, P], BF16)
        o_tb = c_in[:, :, :].rearrange("p a (b c) -> p (a b) c", c=P)
        rinv_b = sb("rinv_b", [P, QB, 4])
        qflat = qt_b[:, :, :, :].rearrange("p a b c -> p (a b c)").bitcast(F32)
        on_b = qflat[:, 0:QB * P].rearrange("p (i g d) -> p i g d", i=QB, g=KVB)
        o_fb = qflat[:, QB * P:QB * P + G * N].rearrange("p (h n) -> p h n", h=G)
        mv_b = sb("mv_b", [P, T, 2])
        rs_b = sb("rs_b", [P, 2, T])
        x2 = sb("x2", [P, T, C])
        router_nat = x2[0:E, 0, :]
        x2_t = sb("x2_t", [P, KT, N])

        g_c = sb("g_c", [P, 12, T, E])
        gs_c = sb("gs_c", [P, 6, T])
        gm = sb("gm", [P, T, P])
        gm_t = sb("gm_t", [P, T, P])
        mv_c = sb("mv_c", [P, T, 2])
        rs_c = sb("rs_c", [P, 2, T])
        z_c = x2

        ps = ctx.enter_context(nc.psum_tensor("ps", [P, 8, 512], F32))
        bank = lambda k: ps[:, k, :]
        bankb = lambda k: ps[:, k, :].bitcast(BF16)

        raw = [p_b[:, n, :, :] for n in range(2)]
        qt_flat = qt_b[:, :, :, :].rearrange("p a b c -> p (a b c)")
        sgn = [qt_flat[:, n * KT * C:(n + 1) * KT * C]
               .rearrange("p (a b) -> p a b", a=KT) for n in range(2)]

        const_in = Signal("const_in", 0)
        raw_in = [Signal(f"raw_in{n}", 0) for n in range(2)]
        rout_in = Signal("rout_in", 0)
        w_in = Signal("w_in", 0)
        late_in = Signal("late_in", 0)
        eye_in = Signal("eye_in", 0)
        zeroed = Signal("zeroed", 0)
        signed = Signal("signed", 0)
        summed = Signal("summed", 0)
        turned = Signal("turned", 0)
        kept = Signal("kept", 0)
        total = Signal("total", 0)
        scaled = Signal("scaled", 0)

        x_here = Signal("x_here", 16)
        x_scaled = Signal("x_scaled", 1)
        x_kept = Signal("x_kept", 1)
        a_max = Signal("a_max", 1)
        x_round = Signal("x_round", 1)
        xq_turn = Signal("xq_turn", 1)
        xq_here = Signal("xq_here", 1)
        qkv_full = Signal("qkv_full", 6)
        nat_here = Signal("nat_here", 6)
        t8_here = Signal("t8_here", 6)
        vt_turn = Signal("vt_turn", 2)
        vt_here = Signal("vt_here", 2)
        qt_turn = Signal("qt_turn", 1)
        qt_here = Signal("qt_here", 1)
        bd_here = Signal("bd_here", 2)
        kv_full = Signal("kv_full", 1)
        kv_here = Signal("kv_here", 1)
        s_full = Signal("s_full", 4)
        s_max = Signal("s_max", 4)
        m_parts = Signal("m_parts", 2)
        m_turn = Signal("m_turn", 2)
        m_here = Signal("m_here", 2)
        st_full = Signal("st_full", 8)
        pa_here = Signal("pa_here", 8)
        oa_full = Signal("oa_full", 2)
        rec_full = Signal("rec_full", 1)
        outa_here = Signal("outa_here", 2)
        sq_here = Signal("sq_here", 2)
        ms_here = Signal("ms_here", 1)
        rms_here = Signal("rms_here", 1)
        b_max = Signal("b_max", 1)
        o_scaled = Signal("o_scaled", 1)
        o_round = Signal("o_round", 1)
        oq_turn = Signal("oq_turn", 1)
        oq_here = Signal("oq_here", 1)
        pr_full = Signal("pr_full", 2)
        za_here = Signal("za_here", 2)
        va_here = Signal("va_here", 1)
        ra_here = Signal("ra_here", 1)
        x1_here = Signal("x1_here", 2)
        x1_turn = Signal("x1_turn", 2)
        x1t_here = Signal("x1t_here", 2)

        c_here = Signal("c_here", 16)
        c_turn = Signal("c_turn", 2)
        ct_here = Signal("ct_here", 2)
        v_full = Signal("v_full", 1)
        v_here = Signal("v_here", 1)
        q_full = Signal("q_full", 4)
        q_first = Signal("q_first", 4)
        q_read = Signal("q_read", 4)
        q_slots = Signal("q_slots", 4)
        qb_turn = Signal("qb_turn", 12)
        qb_act = Signal("qb_act", 8)
        kb_dve = Signal("kb_dve", 4)
        sb_full = Signal("sb_full", 16)
        sb_max = Signal("sb_max", 16)
        mb_parts = Signal("mb_parts", 1)
        mb_turn = Signal("mb_turn", 1)
        mb_here = Signal("mb_here", 1)
        mb_sent = Signal("mb_sent", 16 * 6)
        stb_full = Signal("stb_full", 32)
        pb_here = Signal("pb_here", 32)
        pv_done = Signal("pv_done", 8)
        ob_here = Signal("ob_here", 2)
        ob_turn = Signal("ob_turn", 2)
        on_here = Signal("on_here", 2)
        of_turn = Signal("of_turn", 1)
        of_here = Signal("of_here", 1)
        wo_full = Signal("wo_full", 2)
        zb_here = Signal("zb_here", 2)
        vb_here = Signal("vb_here", 1)
        rb_here = Signal("rb_here", 1)
        x2_here = Signal("x2_here", 2)
        x2_turn = Signal("x2_turn", 2)
        x2t_here = Signal("x2t_here", 2)

        rl_full = Signal("rl_full", 1)
        lg_here = Signal("lg_here", 1)
        ex_here = Signal("ex_here", 1)
        gm_here = Signal("gm_here", 1)
        gm_turn = Signal("gm_turn", 1)
        gmt_here = Signal("gmt_here", 1)
        x2_kept = Signal("x2_kept", 1)
        ff_full = Signal("ff_full", 2)
        zc_here = Signal("zc_here", 2)
        vc_here = Signal("vc_here", 1)
        rc_here = Signal("rc_here", 1)
        y_here = Signal("y_here", 1)
        y_sent = Signal("y_sent", 16)
        x_max = Signal("x_max", 1)
        pv_scaled = Signal("pv_scaled", 1)
        gate_sum = Signal("gate_sum", 3)

        carry = {n: ctx.enter_context(nc.semaphore("carry_" + n)) for n in ("pe", "dve", "pool")}

        def carried(eng, n):
            eng.sem_inc(carry[n], 1)

        ch = {n: Chain("ch_" + n, k) for n, k in dict(a1=2, a2=12, a3=4, a4=3, b1=4, b2=3, b3=2, b4=3, c1=15, c2=3).items()}

        block = ctx.enter_context(nc.Block())
        xv = d["x"].rearrange("b (t p) c -> b p t c", p=P)
        cv = d["ctx_2048"].rearrange("b (t p) c -> b p t c", p=P)
        ov = out.rearrange("b (t p) c -> b p t c", p=P)
        one = lambda v, b: v[bass.ds(b, 1), :, :, :].rearrange("a p t c -> p (a t) c")

        NEXT, A, B, C_ = -1, 0, 1, 2

        def run(eng, stages, late=None):
            def step(i):
                if late and isinstance(i, int) and i == 0:
                    late()
                for lag, stage in stages:
                    if not isinstance(i, int) or 0 <= i - lag < NB:
                        stage(i - lag)

            for i in range(-1, 2):
                step(i)
            with eng.Fori(2, NB - 1) as i:
                step(i)
            for i in range(NB - 1, NB + 2):
                step(i)

        @block.sync
        def _(sp):
            pieces = [d["L0_attn_qkv_w"][n * C:(n + 1) * C, :] for n in range(3)] + [d["L0_attn_proj_w"], d["L0_ffn_base_w"]]

            def raw_load(n):
                if n >= 2:
                    sp.wait_ge(signed.sem, n - 1)
                    sp.wait_ge(summed.sem, n - 1)
                sp.dma_start(raw[n % 2], pieces[n].rearrange("(a p) c -> p a c", p=P)).then_inc(raw_in[n % 2].sem, 16)

            row = lambda a: a.rearrange("(a n) -> a n", a=1)
            raw_load(0)
            raw_load(1)
            sp.dma_start(cf[:, :], d["const_f"]).then_inc(const_in.sem, 16)
            early = [
                (qkv_bias[:, :], row(d["L0_attn_qkv_b"]).to_broadcast([P, 3 * C])),
                (proj_bias[:, :], row(d["L0_attn_proj_b"]).to_broadcast([P, C])),
                (norm_w[:, :], row(d["L0_attn_norm_w"]).to_broadcast([P, C])),
                (base_bias[:, :], row(d["L0_ffn_base_b"]).to_broadcast([P, C])),
                (router_bias[:, :], row(d["L0_ffn_router_b"]).to_broadcast([P, E])),
                (maxt_a[:, :], d["const_b"][:, b_at["maxt0"][0]:b_at["maxt0"][0] + P]),
            ]
            assert len(early) == EARLY
            for n, (dst, src) in enumerate(early):
                if n == 1:
                    raw_load(2)
                sp.dma_start(dst, src).then_inc(w_in.sem, 16)
            raw_load(3)

            def late():
                raw_load(4)
                sp.dma_start(router_nat[:, :], d["L0_ffn_router_w"]).then_inc(rout_in.sem, 16)
                loads = [(wkv[:, n, :, :], d["L0_xattn_" + w].rearrange("(k p) n -> p k n", p=P))
                         for n, w in enumerate(("Wsk", "Wk", "Wsv", "Wv"))]
                loads += [(wq[:, :, :], d["L0_xattn_Wq"].rearrange("(k p) n -> p k n", p=P)),
                          (lora_b[:, :], d["L0_ffn_lora_B"].rearrange("e r n -> (e r) n"))]
                for k in range(KVB):
                    loads.append((wo[k * DB:(k + 1) * DB, :, :],
                                  d["L0_xattn_Wo"][k * G * DB:(k + 1) * G * DB, :].rearrange("(h d) n -> d h n", d=DB)))
                for k in range(KT):
                    loads.append((rl[:, k, E:].rearrange("p (e r) -> p e r", e=E),
                                  d["L0_ffn_lora_A"][:, k * P:(k + 1) * P, :].rearrange("e p r -> p e r")))
                assert len(loads) == LATE
                for dst, src in loads:
                    sp.dma_start(dst, src).then_inc(late_in.sem, 16)

            def a0(b):
                x_kept.before(sp, b)
                x_scaled.before(sp, b)
                a_max.before(sp, b)
                sp.dma_start(x_in[:, :, :], one(xv, b)).then_inc(x_here.sem, 16)

            def b1(b):
                ob_turn.before(sp, b)
                sp.dma_start(c_in[:, :, :], one(cv, b)).then_inc(c_here.sem, 16)

            def b2(b):
                mb_here(sp, b)
                sb_max(sp, b)
                for half in range(2):
                    for p in range(3):
                        sp.dma_start(
                            qt_b[96 + p:97 + p, half * 4:half * 4 + 4, :, :].rearrange("p i g q -> p (i g) q"),
                            maxt_b[p * S:(p + 1) * S, half, :]).then_inc(mb_sent.sem, 16)

            def c2(b):
                y_here(sp, b)
                sp.dma_start(one(ov, b), z_c[:, :, :]).then_inc(y_sent.sem, 16)

            run(sp, [(NEXT, a0), (B, b2), (C_, c2), (A, b1)], late)
            y_sent(sp, NB - 1)

        W_IN, LATE_IN = 16 * EARLY, 16 * LATE

        @block.gpsimd
        def _(pool):
            pool.memset(kv_bd[:, :, :], 0.0).then_inc(zeroed.sem, 1)
            pool.memset(v_b[:, :, :, :], 0.0).then_inc(zeroed.sem, 1)
            pool.wait_ge(zeroed.sem, 2)
            pool.memset(v_b[:, :, :, DB:DB + 1], 1.0).then_inc(zeroed.sem, 1)
            pool.wait_ge(zeroed.sem, 3)
            pool.wait_ge(w_in.sem, W_IN)
            pool.wait_ge(const_in.sem, 32)

            def a0(b):
                a_max(pool, b)
                x_here(pool, b)
                x_round.before(pool, b)
                o_round.before(pool, b)
                carried(pool, "pool")
                for t in range(T):
                    ins = pool.tensor_scalar(y_a[:, t, :], x_in[:, t, :], st_a[:, 1, t:t + 1], 127.0, ALU.mult, ALU.mult)
                ins.then_inc(x_scaled.sem, 1)

            def a1(b):
                za_here.before(pool, b)
                for t in range(T):
                    ins = pool.tensor_tensor(x_res[:, t, :], x_in[:, t, :], proj_bias[:, :], ALU.add)
                ins.then_inc(x_kept.sem, 1)
                for t in range(T):
                    t8_here(pool, b, 3 * t + 1)
                    if t:
                        st_full(pool, b, 4)
                    else:
                        st_full.before(pool, b)
                    carried(pool, "pool")
                    for s in range(HT):
                        ins = pool.tensor_scalar(q_bd[:, :, s, :], q8[:, t, :, :].rearrange("p (c n) h -> p c (n h)", c=4), strip[:, s:s + 1], 1.0, ALU.mult, ALU.mult)
                    ins.then_inc(bd_here.sem, 1)

            def a3(b):
                ms_here(pool, b)
                pool.tensor_tensor(rs_a[:, 1, :], rs_a[:, 0, :], neghalf, ALU.pow).then_inc(rms_here.sem, 1)
                b_max(pool, b)
                x_round(pool, b)
                carried(pool, "pool")
                for t in range(T):
                    ins = pool.tensor_scalar(y_a[:, t, :], out_a[:, t, :], st_a[:, 5, t:t + 1], 127.0, ALU.mult, ALU.mult)
                ins.then_inc(o_scaled.sem, 1)

            def a4(b):
                va_here(pool, b)
                pool.tensor_tensor(rs_a[:, 3, :], rs_a[:, 2, :], neghalf, ALU.pow).then_inc(ra_here.sem, 1)

            def b4(b):
                vb_here(pool, b)
                pool.tensor_tensor(rs_b[:, 1, :], rs_b[:, 0, :], neghalf, ALU.pow).then_inc(rb_here.sem, 1)

            def c1(b):
                x2_turn(pool, b)
                for t in range(T):
                    ins = pool.tensor_tensor(z_c[:, t, :], x2[:, t, :], base_bias[:, :], ALU.add)
                ins.then_inc(x2_kept.sem, 1)

            def c2(b):
                vc_here(pool, b)
                pool.tensor_tensor(rs_c[:, 1, :], rs_c[:, 0, :], neghalf, ALU.pow).then_inc(rc_here.sem, 1)

            run(pool, [(A, a1), (C_, c1), (A, a3), (NEXT, a0), (C_, c2), (A, a4), (B, b4)])

        @block.scalar
        def _(act):
            act.dma_start(cb[:, 0:P], d["const_b"][:, 0:P]).then_inc(eye_in.sem, 16)
            act.dma_start(cb[:, P:], d["const_b"][:, P:]).then_inc(const_in.sem, 16)
            for n in range(4):
                act.wait_ge(raw_in[n % 2].sem, 16 * (n // 2 + 1))
                if n >= 2:
                    act.wait_ge(turned.sem, n - 1)
                act.activation(sgn[n % 2], raw[n % 2], ACT.Sign).then_inc(signed.sem, 1)
            for n in range(3):
                act.wait_ge(turned.sem, n + 1)
                act.activation(qkv_sign[:, :, n * C:(n + 1) * C].rearrange("p k (j o) -> p k j o", j=4),
                               ps[:, 2 * n:2 * n + 2, :].bitcast(BF16).rearrange("p b (k j o) -> p (b k) j o", k=2, j=4),
                               ACT.Copy).then_inc(kept.sem, 1)
            act.wait_ge(turned.sem, 4)
            act.activation(proj_sign[:, :, :].rearrange("p k (j o) -> p k j o", j=4),
                           ps[:, 6:8, :].bitcast(BF16).rearrange("p b (k j o) -> p (b k) j o", k=2, j=4),
                           ACT.Copy).then_inc(kept.sem, 1)

            def late():
                act.wait_ge(turned.sem, 5)
                act.activation(rl[:, :, 0:E], ps[:, 4, 0:KT * E].rearrange("p (k e) -> p k e", e=E), ACT.Copy).then_inc(kept.sem, 1)
                act.wait_ge(turned.sem, 6)
                act.activation(base_t[:, :, :], ps[:, 4:8, :], ACT.Copy).then_inc(kept.sem, 1)

            def a1(b):
                xq_turn(act, b)
                pr_full.before(act, b)
                act.activation(xq_t[:, :, :].rearrange("p k (t n) -> p t k n", t=T),
                               bankb(0).rearrange("p (t k n) -> p t k n", t=T, k=KT), ACT.Copy).then_inc(xq_here.sem, 1)

            def a1_q(b):
                qt_turn(act, b)
                act.activation(q_t[:, :, :], bank(1).rearrange("p (k n) -> p k n", k=KT), ACT.Copy).then_inc(qt_here.sem, 1)

            def a1_v(b):
                vt_turn(act, b)
                for t in range(T):
                    act.activation(v8t[t].rearrange("p (c a) d -> p a c d", a=HT),
                                   ps[:, 0:4, t * P:(t + 1) * P].rearrange("p a (c d) -> p a c d", c=4), ACT.Copy).then_inc(vt_here.sem, 1)

            def a2_m(b, t):
                m_turn(act, b, t + 1)
                act.activation(maxt_a[0:3 * GRP, :], bankb(3)[0:3 * GRP, 0:P], ACT.Copy).then_inc(m_here.sem, 1)

            def a2_x(b, t, quarters):
                for c in quarters:
                    st_full(act, b, 4 * t + c + 1)
                    if c == 0 and t == 1:
                        oa_full(act, b, 1)
                    act.activation(p_a[:, c * HT:(c + 1) * HT, :], bank(c).rearrange("p (h n) -> p h n", h=HT),
                                   ACT.Exp, scale=DA ** -0.5).then_inc(pa_here.sem, 1)

            def a3_sq(b, t):
                outa_here(act, b, t + 1)
                act.activation(nat[:, t, 0, :], out_a[:, t, :], ACT.Square,
                               accum_out=st_a[:, 3, t:t + 1]).then_inc(sq_here.sem, 1)

            def a3_t(b):
                oq_turn(act, b)
                act.activation(xq_t[:, :, :].rearrange("p k (t n) -> p t k n", t=T),
                               bankb(0).rearrange("p (t k n) -> p t k n", t=T, k=KT), ACT.Copy).then_inc(oq_here.sem, 1)

            def b1_x1(b):
                for t in range(T):
                    x1_turn(act, b, t + 1)
                    act.activation(x1_t[:, :, t * P:(t + 1) * P], bank(6 + t).rearrange("p (k n) -> p k n", k=KT),
                                   ACT.Copy).then_inc(x1t_here.sem, 1)

            def b1_c(b):
                for t in range(T):
                    c_turn(act, b, t + 1)
                    act.activation(c_t[:, :, t * P:(t + 1) * P], bank(4 + t).rearrange("p (k n) -> p k n", k=KT),
                                   ACT.Copy).then_inc(ct_here.sem, 1)

            def b1_k(b, t):
                q_full(act, b, 2 * t + 1)
                if t:
                    qb_turn(act, b, 2)
                else:
                    qb_turn.before(act, b)
                act.activation(kn[:, :, :, 0:DB], bank(4)[:, 0:2 * P].rearrange("p (s g d) -> p s g d", s=2, g=KVB),
                               ACT.Copy).then_inc(q_first.sem, 1)

            def b1_q(b, t):
                q_full(act, b, 2 * t + 2)
                if t:
                    qb_turn(act, b, 6)
                act.activation(qn[:, :, 0:DB], bank(5).rearrange("p (h d) -> p h d", d=DB),
                               ACT.Copy).then_inc(q_first.sem, 1)

            def b1_keep(b, t):
                for n in range(4):
                    qb_turn(act, b, 6 * t + 2 + n + 1)
                    act.activation(qt_b[:, 4 * t:4 * t + 4, 2 * n:2 * n + 2, :].rearrange("p i g q -> p g i q"),
                                   bankb(6 + n % 2).rearrange("p (g i q) -> p g i q", g=2, i=4),
                                   ACT.Copy).then_inc(qb_act.sem, 1)

            def b2(b):
                mb_turn(act, b)
                act.activation(maxt_b[:, :, :], bankb(4)[0:3 * S, 0:2 * P].rearrange("p (a q) -> p a q", a=2),
                               ACT.Copy).then_inc(mb_here.sem, 1)

            def b3(b, m, half):
                r, j = m // KB, m % KB
                if m >= 2 and half == 0:
                    pv_done(act, b, m - 1)
                cols = 4 * P if j < KB - 1 else 2 * P
                for s in (2 * half, 2 * half + 1):
                    n = 4 * m + s
                    stb_full(act, b, n + 1)
                    act.activation(p_b[:, j % 2, s, 0:cols], bank(4 + n % 2)[:, 0:cols], ACT.Exp,
                                   scale=DB ** -0.5).then_inc(pb_here.sem, 1)

            def b3_keep(b, r):
                pv_done(act, b, KB * r + KB)
                if r:
                    ob_turn(act, b, 1)
                act.activation(o_tb[:, :, :], ps[:, 6:8, :].rearrange("p b (i n) -> p (b i) n", i=4),
                               ACT.Copy).then_inc(ob_here.sem, 1)

            def b4(b):
                of_turn(act, b)
                act.activation(o_fb[:, :, :].rearrange("p h (i q) -> p i h q", q=S),
                               ps[:, 6:8, :].rearrange("p b (i h q) -> p (b i) h q", h=G, q=S), ACT.Copy).then_inc(of_here.sem, 1)

            def c1_x2(b):
                for t in range(T):
                    x2_turn(act, b, t + 1)
                    act.activation(x2_t[:, :, t * P:(t + 1) * P], bank(6 + t).rearrange("p (k n) -> p k n", k=KT),
                                   ACT.Copy).then_inc(x2t_here.sem, 1)

            def c1(b):
                lg_here(act, b)
                act.activation(g_c[:, 2, :, :], g_c[:, 1, :, :], ACT.Exp).then_inc(ex_here.sem, 1)

            def c2(b):
                gm_turn(act, b)
                act.activation(gm_t[:, :, :], bank(0)[:, 0:2 * P].rearrange("p (t n) -> p t n", t=T), ACT.Copy).then_inc(gmt_here.sem, 1)

            of = lambda f, n: lambda b: f(b, n)
            of = lambda f, *n: lambda b: f(b, *n)
            exps = lambda m: [(B, of(b3, m, 0)), (B, of(b3, m, 1))]
            run(act, [(B, b1_c), (C_, c1_x2), (B, b1_x1), (C_, c1), (A, a1_q), (B, of(b1_k, 0)), (B, of(b1_q, 0)),
                      (A, a1_v), (B, of(b1_k, 1)), (B, of(b1_keep, 0)), (B, of(b1_q, 1)), (B, of(b1_keep, 1)),
                      (A, of(a2_m, 0)), (A, of(a2_x, 0, range(4))), (A, of(a3_sq, 0)), (A, of(a2_m, 1)), (A, of(a2_x, 1, range(3))),
                      (B, b2), (A, of(a2_x, 1, [3]))] + exps(0) + [(A, of(a3_sq, 1)), (C_, c2)] + exps(1) + exps(2) + exps(3) + [(A, a3_t)]
                + [(B, of(b3, 4, 0)), (B, of(b3_keep, 0)), (B, of(b3, 4, 1))] + exps(5) + exps(6) + exps(7)
                + [(B, of(b3_keep, 1)), (NEXT, a1), (B, b4)], late)

        @block.tensor
        def _(pe):
            pe.wait_ge(eye_in.sem, 16)
            for n in range(4):
                pe.wait_ge(signed.sem, n + 1)
                for k in range(KT):
                    for j in range(4):
                        mm = pe.transpose(bankb(2 * n + k // 2)[:, (k % 2) * C + j * P:(k % 2) * C + (j + 1) * P],
                                          sgn[n % 2][:, j, k * P:(k + 1) * P], eyeb)
                mm.then_inc(turned.sem, 1)
            pe.wait_ge(const_in.sem, 32)
            pe.wait_ge(kept.sem, 2)
            pe.wait_ge(summed.sem, 4)
            pe.matmul(bank(3)[:, 0:4], ones, abs_sums[:, :], start=True, stop=True).then_inc(total.sem, 1)
            pe.wait_ge(kept.sem, 4)
            pe.wait_ge(scaled.sem, 5)
            pe.wait_ge(w_in.sem, W_IN)
            pe.wait_ge(zeroed.sem, 3)

            def late():
                pe.wait_ge(rout_in.sem, 16)
                for k in range(KT):
                    mm = pe.transpose(bank(4)[:, k * E:(k + 1) * E], router_nat[0:E, k * P:(k + 1) * P], eye[0:E, 0:E])
                mm.then_inc(turned.sem, 1)
                pe.wait_ge(kept.sem, 5)
                pe.wait_ge(raw_in[0].sem, 48)
                for k in range(KT):
                    for j in range(4):
                        mm = pe.transpose(bank(4 + k)[:, j * P:(j + 1) * P], raw[0][:, j, k * P:(k + 1) * P], eye)
                mm.then_inc(turned.sem, 1)
                pe.wait_ge(kept.sem, 6)
                pe.wait_ge(late_in.sem, LATE_IN)

            def a1(b):
                x_round(pe, b)
                if not (isinstance(b, int) and b < 2):
                    on_here(pe, b - 2, 1)
                for t in range(T):
                    for k in range(KT):
                        mm = pe.transpose(bankb(0)[:, t * C + k * P:t * C + (k + 1) * P], xq[:, t, k * P:(k + 1) * P], eyeb)
                mm.then_inc(xq_turn.sem, 1)

            def a1_qkv(b, t, which=range(3)):
                if t == 0 and 0 in which:
                    xq_here(pe, b)
                    za_here.before(pe, b)
                for w in which:
                    if t:
                        nat_here(pe, b, w + 1)
                    for k in range(KT):
                        mm = pe.matmul(bank(1 + w), xq_t[:, k, t * P:(t + 1) * P], qkv_sign[:, k, w * C:(w + 1) * C],
                                       start=(k == 0), stop=(k == KT - 1))
                    mm.then_inc(qkv_full.sem, 1)

            def a1_state(b):
                nat_here(pe, b, 4)
                for k in range(KT):
                    mm = pe.transpose(bank(1)[:, k * P:(k + 1) * P], nat[:, 1, 0, k * P:(k + 1) * P], eye)
                mm.then_inc(qt_turn.sem, 1)
                nat_here(pe, b, 5)
                for k in range(KT):
                    mm = pe.matmul(bank(2)[:, k * P:(k + 1) * P], nat[:, 0, 1, k * P:(k + 1) * P], nat[:, 0, 2, k * P:(k + 1) * P],
                                   start=True, stop=True)
                mm.then_inc(kv_full.sem, 1)

            def a1_v(b, t):
                if t == 0:
                    qt_here(pe, b)
                    kv_here(pe, b)
                    if not (isinstance(b, int) and b < 2):
                        gm_here(pe, b - 2)
                t8_here(pe, b, 3 * t + 3)
                carried(pe, "pe")
                for j in range(GRP):
                    c, a = j // HT, j % HT
                    mm = pe.transpose(bank(a)[:, (t * 4 + c) * DA:(t * 4 + c + 1) * DA],
                                      v8[a * S:(a + 1) * S, c * TOK:(c + 1) * TOK, :].rearrange("p n h -> p (n h)"),
                                      eye[a * S:(a + 1) * S, a * S:(a + 1) * S])
                mm.then_inc(vt_turn.sem, 1)

            def a2_s(b, t, quarters):
                bd_here(pe, b, t + 1)
                t8_here(pe, b)
                if t == 0:
                    vt_here(pe, b)
                for c in quarters:
                    if t and c == 0:
                        outa_here(pe, b, 1)
                    pe.matmul(bank(c), tokhot, other, start=True, stop=False)
                    for a in range(HT):
                        mm = pe.matmul(bank(c)[:, a * P:(a + 1) * P], q_bd[:, c, a, :],
                                       k8[:, t, c * TOK:(c + 1) * TOK, :].rearrange("p n h -> p (n h)"),
                                       start=False, stop=(a == HT - 1))
                    if c % 2:
                        mm.then_inc(s_full.sem, 1)

            def a2_m(b, t):
                m_parts(pe, b, t + 1)
                carried(pe, "pe")
                pe.transpose(bankb(3)[0:3 * GRP, 0:P], maxp_a[:, :, :].rearrange("p a h -> p (a h)"), eyeb).then_inc(m_turn.sem, 1)

            def a2_x(b, t, quarters):
                m_here(pe, b, t + 1)
                for c in quarters:
                    for a in range(HT):
                        pe.matmul(bank(c)[:, a * P:(a + 1) * P], sel[0:3 * GRP + TOK, c * HT + a, :], maxt_a[0:3 * GRP + TOK, :],
                                  start=(a == 0), stop=False)
                    pe.matmul(bank(c), k8[:, t, c * TOK:(c + 1) * TOK, :].rearrange("p n h -> p (n h)"),
                              q_bd[:, c, :, :].rearrange("p a n -> p (a n)"), start=False, stop=True).then_inc(st_full.sem, 1)

            def a2_v(b, t):
                for c in range(4):
                    pa_here(pe, b, 4 * t + max(c + 1, 2))
                    for a in range(HT):
                        pe.matmul(bank(0)[a * S:(a + 1) * S, c * P:(c + 1) * P], v8t[t][:, c * HT + a, :],
                                  p_a[:, c * HT + a, :], start=True, stop=True)
                    for a in range(HT):
                        mm = pe.matmul(bank(1)[a * S:(a + 1) * S, c * P:(c + 1) * P], ones[:, 0:S], p_a[:, c * HT + a, :],
                                       start=True, stop=True)
                mm.then_inc(oa_full.sem, 1)
                if t == 1:
                    for f in range(KT):
                        mm = pe.matmul(bank(2)[:, f * P:(f + 1) * P], q_t[:, f, :], kv_bd[:, f, :], start=True, stop=True)
                    mm.then_inc(rec_full.sem, 1)

            def a3_t(b):
                o_round(pe, b)
                for t in range(T):
                    for k in range(KT):
                        mm = pe.transpose(bankb(0)[:, t * C + k * P:t * C + (k + 1) * P], xq[:, t, k * P:(k + 1) * P], eyeb)
                mm.then_inc(oq_turn.sem, 1)

            def a3(b, t):
                if t == 0:
                    if not (isinstance(b, int) and b < 2):
                        zc_here(pe, b - 2)
                    oq_here(pe, b)
                for k in range(KT):
                    mm = pe.matmul(bank(1 + t), xq_t[:, k, t * P:(t + 1) * P], proj_sign[:, k, :], start=(k == 0), stop=(k == KT - 1))
                mm.then_inc(pr_full.sem, 1)

            def b1_x1(b):
                x2t_here.before(pe, b)
                for t in range(T):
                    x1_here(pe, b, t + 1)
                    for k in range(KT):
                        mm = pe.transpose(bank(6 + t)[:, k * P:(k + 1) * P], x1[:, t, k * P:(k + 1) * P], eye)
                    mm.then_inc(x1_turn.sem, 1)

            def b1_c(b):
                c_here(pe, b)
                zb_here.before(pe, b)
                for t in range(T):
                    for k in range(KT):
                        mm = pe.transpose(bank(4 + t)[:, k * P:(k + 1) * P], c_in[:, t, k * P:(k + 1) * P], eye)
                    mm.then_inc(c_turn.sem, 1)

            def b1_v(b):
                ct_here(pe, b)
                x1t_here(pe, b)
                for j in range(KB):
                    for k in range(KT):
                        for s in range(4):
                            c, src = s // 2, s % 2
                            src_t = (c_t, x1_t)[src]
                            at = 64 * j + S * c
                            mm = pe.matmul(bank(6)[s * S:(s + 1) * S, j * P:(j + 1) * P], src_t[:, k, at:at + S], wkv[:, 2 + src, k, :],
                                           start=(k == 0), stop=(k == KT - 1))
                mm.then_inc(v_full.sem, 1)

            def b1_k(b, t):
                if t:
                    q_read(pe, b, 1)
                for src in range(2):
                    src_t = (c_t, x1_t)[src]
                    for k in range(KT):
                        mm = pe.matmul(bank(4)[:, src * P:(src + 1) * P], src_t[:, k, t * P:(t + 1) * P], wkv[:, src, k, :],
                                       start=(k == 0), stop=(k == KT - 1))
                mm.then_inc(q_full.sem, 1)

            def b1_q(b, t, ks=range(2 * KT)):
                if t and 0 in ks:
                    q_read(pe, b, 2)
                for k in ks:
                    src_t = (c_t, x1_t)[k // KT]
                    mm = pe.matmul(bank(5), src_t[:, k % KT, t * P:(t + 1) * P], wq[:, k, :], start=(k == 0), stop=(k == 2 * KT - 1))
                    if k == 2 * KT - 1:
                        mm.then_inc(q_full.sem, 1)

            def b1_kt(b, t):
                q_slots(pe, b, 2 * t + 1)
                if t == 0:
                    v_here(pe, b)
                for half in range(2):
                    if t:
                        qb_act(pe, b, 3 + half)
                    for g in range(4):
                        for src in range(2):
                            o = bankb(6 + half)[:, g * C // 2:(g + 1) * C // 2].rearrange("p (c s k) -> p c s k", s=2, k=S)[:, :, src, :]
                            mm = pe.transpose(o, kn[:, src, 4 * half + g, :], eyeb)
                    mm.then_inc(qb_turn.sem, 1)

            def b1_qt(b, t, quarters):
                q_slots(pe, b, 2 * t + 2)
                for q in quarters:
                    if q < 2:
                        kb_dve(pe, b, 2 * t + q + 1)
                    else:
                        qb_act(pe, b, 4 * t + q - 1)
                    for g in range(2):
                        for hh in range(G):
                            o = bankb(6 + q % 2)[:, g * C:(g + 1) * C].rearrange("p (i h q) -> p i h q", i=4, h=G)[:, :, hh, :]
                            mm = pe.transpose(o, qn[:, (2 * q + g) * G + hh, :], eyeb)
                    mm.then_inc(qb_turn.sem, 1)

            def b2(b, i):
                if i == 0:
                    qb_act(pe, b)
                    kb_dve(pe, b)
                c0 = max(i - 2, 0)
                cols = (i - c0 + 1) * 2 * S
                for half in range(2):
                    if i:
                        sb_max(pe, b, 2 * i + half - 1)
                    for g in range(4):
                        o = bank(4 + 2 * half + g // 2)[:, (g % 2) * 256:(g % 2) * 256 + cols]
                        gg = 4 * half + g
                        pe.matmul(o, qt_b[:, i, gg, :], kt_b[:, gg, c0:i + 1, :].rearrange("p c k -> p (c k)"), start=True, stop=False)
                        if i < 2:
                            mm = pe.matmul(o[:, cols - 2 * S:cols], rep, mask_nat[:, 1, :], start=False, stop=True)
                        else:
                            mm = pe.matmul(o.rearrange("p (c k) -> p c k", c=3)[:, 0:3:2, :], rep, mask_nat, start=False, stop=True)
                    mm.then_inc(sb_full.sem, 1)

            def b2_max(b):
                mb_parts(pe, b)
                for a in range(2):
                    mm = pe.transpose(bankb(4)[0:3 * S, a * P:(a + 1) * P], maxp_b[:, a, :, :, :].rearrange("p a i g -> p (a i g)"), eyeb)
                mm.then_inc(mb_turn.sem, 1)

            def b3_s(b, m, half):
                if m == 0 and half == 0:
                    mb_here(pe, b)
                    mb_sent(pe, b)
                r, j = m // KB, m % KB
                cols = 4 * P if j < KB - 1 else 2 * P
                for s in (2 * half, 2 * half + 1):
                    g, n = 4 * r + s, 4 * m + s
                    if n >= 2:
                        pb_here(pe, b, n - 1)
                    pe.matmul(bank(4 + n % 2)[:, 0:cols], kt_b[:, g, 2 * j:2 * j + 2, :].rearrange("p c k -> p (c k)"),
                              qt_b[:, 2 * j:2 * j + cols // P, g, :], start=True, stop=False)
                    pe.matmul(bank(4 + n % 2)[:, 0:cols], key, mask_tr[:, 0:cols], start=False, stop=True).then_inc(stb_full.sem, 1)

            def b3_w(b, m):
                r, j = m // KB, m % KB
                pb_here(pe, b, 4 * m + 4)
                if r and j == 0:
                    ob_here(pe, b, 1)
                for half in range(2 if j < KB - 1 else 1):
                    at = 2 * j + 2 * half
                    for s in range(4):
                        mm = pe.matmul(bank(6 + at // 4)[s * S:(s + 1) * S, (at % 4) * P:(at % 4) * P + 2 * P], v_b[:, j, 4 * r + s, :],
                                       p_b[:, j % 2, s, half * 2 * P:(half + 1) * 2 * P],
                                       start=(at == 0 or (j == 1 and half == 1)), stop=True, skip_group_check=True)
                mm.then_inc(pv_done.sem, 1)

            def b3_back(b, r):
                ob_here(pe, b, r + 1)
                for i in range(QB):
                    k = 4 * r + i // 4 if r else 3 * (i // 4)
                    mm = pe.transpose(bank(k)[:, (i % 4) * P:(i % 4 + 1) * P], o_tb[:, i, :], eye)
                mm.then_inc(ob_turn.sem, 1)

            def b4_on(b):
                on_here(pe, b)
                for i in range(QB):
                    mm = pe.transpose(bank(6 + i // 4)[:, (i % 4) * P:(i % 4 + 1) * P], on_b[:, i, :, :].rearrange("p g d -> p (g d)"), eye)
                mm.then_inc(of_turn.sem, 1)

            def b4(b, t):
                of_here(pe, b)
                for k in range(G):
                    mm = pe.matmul(bank(4 + t), o_fb[:, k, t * P:(t + 1) * P], wo[:, k, :], start=(k == 0), stop=(k == G - 1))
                mm.then_inc(wo_full.sem, 1)

            def c1_x2(b):
                for t in range(T):
                    x2_here(pe, b, t + 1)
                    for k in range(KT):
                        mm = pe.transpose(bank(6 + t)[:, k * P:(k + 1) * P], x2[:, t, k * P:(k + 1) * P], eye)
                    mm.then_inc(x2_turn.sem, 1)

            def c1(b):
                x2t_here(pe, b)
                for t in range(T):
                    for k in range(KT):
                        mm = pe.matmul(bank(0)[:, t * 256:t * 256 + E + P], x2_t[:, k, t * P:(t + 1) * P], rl[:, k, :], start=(k == 0), stop=(k == KT - 1))
                mm.then_inc(rl_full.sem, 1)

            def c2_gates(b):
                zc_here.before(pe, b)
                if isinstance(b, int) and b + 2 >= NB:
                    za_here(pe, NB - 1)
                else:
                    outa_here(pe, b + 2)
                gm_here(pe, b)
                for t in range(T):
                    mm = pe.transpose(bank(0)[:, t * P:(t + 1) * P], gm[:, t, :], eye)
                mm.then_inc(gm_turn.sem, 1)

            def c2(b, t, half):
                for k in (2 * half, 2 * half + 1):
                    pe.matmul(bank(1 + t), x2_t[:, k, t * P:(t + 1) * P], base_t[:, k, :], start=(k == 0), stop=False)
                if half:
                    if t == 0:
                        gmt_here(pe, b)
                    pe.matmul(bank(1 + t), gm_t[:, t, :], lora_b[:, :], start=False, stop=True).then_inc(ff_full.sem, 1)

            of = lambda f, n: lambda b: f(b, n)
            of = lambda f, *n: lambda b: f(b, *n)

            def attend(m, *between):
                return [(B, of(b3_s, m, 0)), (B, of(b3_w, m - 1)), (B, of(b3_s, m, 1)), *between]

            run(pe, [(B, b1_c), (A, of(a1_qkv, 1)), (C_, c1_x2), (B, b1_x1), (C_, c1), (B, b1_v),
                     (A, a1_state), (B, of(b1_k, 0)), (B, of(b1_q, 0)), (A, of(a1_v, 0)), (B, of(b1_kt, 0)), (A, of(a1_v, 1)),
                     (B, of(b1_k, 1)), (B, of(b1_q, 1, [0, 1, 2, 3])), (B, of(b1_qt, 0, [0, 1])), (B, of(b1_q, 1, [4, 5])),
                     (B, of(b1_qt, 0, [2])), (B, of(b1_q, 1, [6])), (B, of(b1_qt, 0, [3])), (B, of(b1_q, 1, [7])),
                     (A, of(a2_s, 0, [2])), (B, of(b1_kt, 1)), (A, of(a2_s, 0, [3])), (B, of(b1_qt, 1, [0, 1])),
                     (A, of(a2_s, 0, [0])), (B, of(b1_qt, 1, [2])), (A, of(a2_s, 0, [1])), (B, of(b1_qt, 1, [3])),
                     (B, of(b2, 0)), (A, of(a2_m, 0)), (A, of(a2_x, 0, [0])), (B, of(b2, 1)), (A, of(a2_x, 0, [1])),
                     (B, of(b2, 2)), (A, of(a2_x, 0, [2])), (A, of(a2_x, 0, [3])), (A, of(a2_v, 0)), (B, of(b2, 3)),
                     (A, of(a2_s, 1, [2, 3])), (B, of(b2, 4)), (A, of(a2_s, 1, [0, 1])), (B, of(b2, 5)), (A, of(a2_m, 1)),
                     (A, of(a2_x, 1, [0])), (B, of(b2, 6)),
                     (A, of(a2_x, 1, [1])), (B, of(b2, 7)), (A, of(a2_x, 1, [2])), (B, b2_max), (A, of(a2_x, 1, [3])),
                     (A, of(a2_v, 1)), (B, of(b3_s, 0, 0)), (B, of(b3_s, 0, 1)), (C_, c2_gates)]
                + attend(1, (C_, of(c2, 0, 0))) + attend(2, (C_, of(c2, 0, 1))) + attend(3, (A, a3_t), (C_, of(c2, 1, 0)))
                + attend(4, (C_, of(c2, 1, 1))) + attend(5, (A, of(a3, 0))) + attend(6, (A, of(a3, 1)), (B, of(b3_back, 0)))
                + attend(7)
                + [(B, of(b3_w, 7)), (NEXT, a1), (B, of(b3_back, 1)), (NEXT, of(a1_qkv, 0, [0])), (B, b4_on),
                   (NEXT, of(a1_qkv, 0, [1])), (B, of(b4, 0)), (B, of(b4, 1)), (NEXT, of(a1_qkv, 0, [2]))], late)

        @block.vector
        def _(dve):
            for n in range(4):
                dve.wait_ge(raw_in[n % 2].sem, 16 * (n // 2 + 1))
                dve.tensor_reduce(abs_sums[:, n:n + 1], raw[n % 2], AX.XY, ALU.add, apply_absolute_value=True).then_inc(summed.sem, 1)
            dve.wait_ge(total.sem, 1)
            links = [0]

            def link0(ins):
                links[0] += 1
                ins.then_inc(scaled.sem, 1)
                dve.wait_ge(scaled.sem, links[0])

            link0(dve.tensor_reduce(wscale[:, 2:3], bank(3)[:, 0:3], AX.X, ALU.add))
            link0(dve.tensor_copy(wscale[:, 3:4], bank(3)[:, 3:4]))
            link0(dve.tensor_scalar(wscale[:, 0:1], wscale[:, 2:3], 1.0 / (3 * C * C), 1e-5, ALU.mult, ALU.max))
            link0(dve.tensor_scalar(wscale[:, 1:2], wscale[:, 3:4], 1.0 / (C * C), 1e-5, ALU.mult, ALU.max))
            link0(dve.tensor_scalar(wscale[:, 0:2], wscale[:, 0:2], 1.0 / 127.0, None, ALU.mult))
            dve.wait_ge(const_in.sem, 32)
            dve.wait_ge(zeroed.sem, 3)
            dve.wait_ge(w_in.sem, W_IN)

            def a0(b):
                c = ch["a1"]; c.start(dve, b)
                x_here(dve, b)
                dve.tensor_reduce(st_a[:, 7, :], x_in[:, :, :], AX.X, ALU.max, apply_absolute_value=True).then_inc(x_max.sem, 1)
                x_max(dve, b)
                c.link(dve.tensor_scalar(st_a[:, 0, :], st_a[:, 7, :], 1e-5, None, ALU.max))
                dve.reciprocal(st_a[:, 1, :], st_a[:, 0, :]).then_inc(a_max.sem, 1)
                c.link(dve.tensor_scalar(st_a[:, 2, :], st_a[:, 0, :], wscale[:, 0:1], None, ALU.mult))
                c.end()

            def a0_round(b):
                x_scaled(dve, b)
                oq_turn.before(dve, b)
                dve.tensor_scalar(xq[:, :, :], y_a[:, :, :], MAGIC, MAGIC, ALU.add, ALU.subtract).then_inc(x_round.sem, 1)

            def a1_nat(b, t, which=range(3)):
                for w in which:
                    qkv_full(dve, b, 3 * t + w + 1)
                    dve.scalar_tensor_tensor(nat[:, t, w, :], bank(1 + w), st_a[:, 2, t:t + 1], qkv_bias[:, w * C:(w + 1) * C],
                                             ALU.mult, ALU.add).then_inc(nat_here.sem, 1)

            def a1_t8(b, t, which):
                if t == 0:
                    x1_here.before(dve, b)
                for w in which:
                    dst = (q8[:, t, :, :], k8[:, t, :, :], v8[:, :, :])[w]
                    nat_here(dve, b, 3 * t + w + 1)
                    if t and w == 2:
                        vt_turn(dve, b, 1)
                    dve.transpose(dst.rearrange("p n h -> p h n"), nat[:, t, w, :].rearrange("p (h d) -> p h d", d=DA)).then_inc(t8_here.sem, 1)

            def a1_state(b):
                kv_full(dve, b)
                for s in range(HT):
                    ins = dve.tensor_copy(kv_bd[s * S:(s + 1) * S, :, s * S:(s + 1) * S],
                                          bank(2)[s * S:(s + 1) * S, :].rearrange("p (k n) -> p k n", k=KT)[:, :, s * S:(s + 1) * S])
                ins.then_inc(kv_here.sem, 1)

            def a2_max(b, t):
                c = ch["a2"]
                if t == 0:
                    c.start(dve, b)
                for n, k in enumerate((2, 0)):
                    s_full(dve, b, 2 * t + n + 1)
                    dve.tensor_reduce(max_a[:, 0, k * HT:(k + 2) * HT], ps[:, k:k + 2, :].rearrange("p b (h n) -> p (b h) n", h=HT),
                                      AX.X, ALU.max).then_inc(s_max.sem, 1)
                s_max(dve, b, 2 * t + 2)
                c.link(dve.tensor_scalar(maxp_a[:, 0, :], max_a[:, 0, :], -1.0, None, ALU.mult))
                c.link(dve.scalar_tensor_tensor(max_a[:, 1, :], max_a[:, 0, :], -1.0, maxp_a[:, 0, :], ALU.mult, ALU.subtract))
                c.link(dve.tensor_copy(maxp_a[:, 1, :], max_a[:, 1, :]))
                dve.tensor_tensor(maxp_a[:, 2, :], max_a[:, 1, :], maxp_a[:, 1, :], ALU.subtract).then_inc(m_parts.sem, 1)

            def a2_out(b, t):
                c = ch["a2"]
                bd_here(dve, b)
                oa_full(dve, b, t + 1)
                back = lambda k: bank(k).rearrange("p (n h) -> p h n", h=HA)
                c.link(dve.transpose(sum_a[:, :, :], back(1)))
                c.link(dve.transpose(out_a[:, t, :].rearrange("p (h d) -> p h d", d=DA), back(0)))
                c.link(dve.reciprocal(rinv_a[:, :], sum_a[:, :, 0]))
                ins = dve.tensor_tensor(out_a[:, t, :].rearrange("p (h d) -> p h d", d=DA),
                                        out_a[:, t, :].rearrange("p (h d) -> p h d", d=DA),
                                        rinv_a[:, :].unsqueeze(2).to_broadcast([P, HA, DA]), ALU.mult)
                if t == 0:
                    ins.then_inc(outa_here.sem, 1)
                else:
                    ins.then_inc(pv_scaled.sem, 1)
                    pv_scaled(dve, b)
                    rec_full(dve, b)
                    dve.tensor_tensor(out_a[:, t, :], bank(2), out_a[:, t, :], ALU.add).then_inc(outa_here.sem, 1)
                    c.end()

            def a3(b):
                c = ch["a3"]; c.start(dve, b)
                sq_here(dve, b)
                dve.tensor_scalar(rs_a[:, 0, :], st_a[:, 3, :], 1.0 / C, EPS_RMS, ALU.mult, ALU.add).then_inc(ms_here.sem, 1)
                rms_here(dve, b)
                for t in range(T):
                    ins = dve.scalar_tensor_tensor(out_a[:, t, :], out_a[:, t, :], rs_a[:, 1, t:t + 1], norm_w[:, :], ALU.mult, ALU.mult)
                c.link(ins)
                c.link(dve.tensor_reduce(st_a[:, 7, :], out_a[:, :, :], AX.X, ALU.max, apply_absolute_value=True))
                c.link(dve.tensor_scalar(st_a[:, 4, :], st_a[:, 7, :], 1e-5, None, ALU.max))
                dve.reciprocal(st_a[:, 5, :], st_a[:, 4, :]).then_inc(b_max.sem, 1)
                c.link(dve.tensor_scalar(st_a[:, 6, :], st_a[:, 4, :], wscale[:, 1:2], None, ALU.mult))
                c.end()
                o_scaled(dve, b)
                xq_turn(dve, b)
                dve.tensor_scalar(xq[:, :, :], y_a[:, :, :], MAGIC, MAGIC, ALU.add, ALU.subtract).then_inc(o_round.sem, 1)

            def a3_z(b):
                x_kept(dve, b)
                for t in range(T):
                    pr_full(dve, b, t + 1)
                    dve.scalar_tensor_tensor(out_a[:, t, :], bank(1 + t), st_a[:, 6, t:t + 1], x_res[:, t, :], ALU.mult, ALU.add).then_inc(za_here.sem, 1)

            def norm_stats(c, z, mv, rs, row, here):
                for t in range(T):
                    c.link(dve.bn_stats(stats[:, t, :], z[:, t, :]))
                carried(dve, "dve")
                for t in range(T):
                    ins = dve.bn_aggr(mv[:, t, :], stats[:, t, :])
                c.link(ins)
                dve.tensor_scalar(rs[:, row, :], mv[:, :, 1], EPS_LN, None, ALU.add).then_inc(here.sem, 1)

            def norm_apply(b, z, mv, rs, row, rstd, dst, done):
                rstd(dve, b)
                for t in range(T):
                    ins = dve.tensor_scalar(dst[:, t, :], z[:, t, :], mv[:, t, 0:1], rs[:, row + 1, t:t + 1], ALU.subtract, ALU.mult)
                    if done.per == T or t == T - 1:
                        ins.then_inc(done.sem, 1)

            def a4_stats(b):
                c = ch["a4"]; c.start(dve, b)
                za_here(dve, b)
                norm_stats(c, out_a, mv_a, rs_a, 2, va_here)
                c.end()

            def a4(b):
                x2_here.before(dve, b)
                norm_apply(b, out_a, mv_a, rs_a, 2, ra_here, x1, x1_here)

            def b1_v(b):
                v_full(dve, b)
                dve.tensor_copy(v_b[:, :, :, 0:DB], bank(6).rearrange("p (j g d) -> p j g d", j=KB, g=KVB)).then_inc(v_here.sem, 1)

            def b1_k(b, t):
                c = ch["b1"]
                if t == 0:
                    c.start(dve, b)
                q_first(dve, b, 2 * t + 1)
                k1 = kn[:, :, :, :].rearrange("p s g c -> p (s g) c")
                kr = k_rest[:, :].rearrange("p (h d) -> p h d", d=DB)
                dve.tensor_copy(k1[:, :, 96:128], kx[:, t:t + 1, :].to_broadcast([P, 2 * KVB, S]))
                dve.tensor_tensor(kr, bank(4)[:, 0:2 * P].rearrange("p (h d) -> p h d", d=DB), k1[:, :, 0:DB], ALU.subtract).then_inc(q_read.sem, 1)
                q_read(dve, b, 2 * t + 1)
                dve.tensor_copy(k1[:, :, 3 * DB:4 * DB], k1[:, :, 0:DB])
                dve.tensor_copy(k1[:, :, 5 * DB:6 * DB], k1[:, :, 0:DB])
                dve.tensor_copy(k1[:, :, 4 * DB:5 * DB], kr)
                c.link(dve.tensor_copy(k1[:, :, DB:2 * DB], kr))
                dve.tensor_tensor(k1[:, :, 2 * DB:3 * DB], kr, k1[:, :, DB:2 * DB], ALU.subtract).then_inc(q_slots.sem, 1)

            def b1_q(b, t):
                c = ch["b1"]
                q_first(dve, b, 2 * t + 2)
                qr = q_rest[:, :].rearrange("p (h d) -> p h d", d=DB)
                dve.tensor_tensor(qr, bank(5).rearrange("p (h d) -> p h d", d=DB), qn[:, :, 0:DB], ALU.subtract).then_inc(q_read.sem, 1)
                q_read(dve, b, 2 * t + 2)
                dve.tensor_copy(qn[:, :, 96:128], qx)
                dve.tensor_copy(qn[:, :, DB:2 * DB], qn[:, :, 0:DB])
                dve.tensor_copy(qn[:, :, 2 * DB:3 * DB], qn[:, :, 0:DB])
                dve.tensor_copy(qn[:, :, 4 * DB:5 * DB], qr)
                c.link(dve.tensor_copy(qn[:, :, 3 * DB:4 * DB], qr))
                dve.tensor_tensor(qn[:, :, 5 * DB:6 * DB], qr, qn[:, :, 3 * DB:4 * DB], ALU.subtract).then_inc(q_slots.sem, 1)
                if t == T - 1:
                    c.end()

            def b1_keep(b, t):
                for n in range(2):
                    qb_turn(dve, b, 6 * t + n + 1)
                    dve.tensor_copy(kt_b[:, 4 * n:4 * n + 4, 4 * t:4 * t + 4, :],
                                    bankb(6 + n).rearrange("p (g c k) -> p g c k", g=4, c=4)).then_inc(kb_dve.sem, 1)

            def b2(b, i):
                cols = (min(i, 2) + 1) * 2 * S
                for half in range(2):
                    sb_full(dve, b, 2 * i + half + 1)
                    dve.tensor_reduce(max_b[:, 0, i, 4 * half:4 * half + 4],
                                      ps[:, 4 + 2 * half:6 + 2 * half, :].rearrange("p b (g n) -> p (b g) n", g=2)[:, :, 0:cols],
                                      AX.X, ALU.max).then_inc(sb_max.sem, 1)

            def b2_max(b):
                c = ch["b2"]; c.start(dve, b)
                sb_max(dve, b)
                m0 = max_b[:, 0, :, :].rearrange("p (a i) g -> p a i g", a=2)
                m1 = max_b[:, 1, :, :].rearrange("p (a i) g -> p a i g", a=2)
                for a in range(2):
                    ins = dve.tensor_scalar(maxp_b[:, a, 0, :, :], m0[:, a], -1.0, None, ALU.mult)
                c.link(ins)
                for a in range(2):
                    ins = dve.scalar_tensor_tensor(m1[:, a], m0[:, a], -1.0, maxp_b[:, a, 0, :, :], ALU.mult, ALU.subtract)
                c.link(ins)
                for a in range(2):
                    ins = dve.tensor_copy(maxp_b[:, a, 1, :, :], m1[:, a])
                c.link(ins)
                for a in range(2):
                    ins = dve.tensor_tensor(maxp_b[:, a, 2, :, :], m1[:, a], maxp_b[:, a, 1, :, :], ALU.subtract)
                ins.then_inc(mb_parts.sem, 1)
                c.end()

            def b3(b, r):
                c = ch["b3"]
                if r == 0:
                    c.start(dve, b)
                else:
                    on_here(dve, b, 1)
                ob_turn(dve, b, r + 1)
                o = [bank(k).rearrange("p (i s c) -> p i s c", i=4, s=4) for k in ((0, 3), (4, 5))[r]]
                for n in range(2):
                    ins = dve.reciprocal(rinv_b[:, 4 * n:4 * n + 4, :], o[n][:, :, :, DB])
                c.link(ins)
                for n in range(2):
                    ins = dve.tensor_tensor(on_b[:, 4 * n:4 * n + 4, 4 * r:4 * r + 4, :], o[n][:, :, :, 0:DB],
                                            rinv_b[:, 4 * n:4 * n + 4, :].unsqueeze(3).to_broadcast([P, 4, 4, DB]), ALU.mult)
                ins.then_inc(on_here.sem, 1)
                if r:
                    c.end()

            def b4_z(b, t):
                wo_full(dve, b, t + 1)
                dve.tensor_tensor(x1[:, t, :], bank(4 + t), x1[:, t, :], ALU.add).then_inc(zb_here.sem, 1)

            def b4(b):
                c = ch["b4"]; c.start(dve, b)
                zb_here(dve, b)
                norm_stats(c, x1, mv_b, rs_b, 0, vb_here)
                c.end()

            def b4_x2(b):
                y_sent.before(dve, b)
                norm_apply(b, x1, mv_b, rs_b, 0, rb_here, x2, x2_here)

            def c1(b):
                c = ch["c1"]; c.start(dve, b)
                rl_full(dve, b)
                wide = lambda r: gs_c[:, r, :].unsqueeze(2).to_broadcast([P, T, E])
                gr = lambda k: g_c[:, k, :, :]
                rmp = ramp.unsqueeze(1).to_broadcast([P, T, E])
                pl = bank(0).rearrange("p (t n) -> p t n", t=T)
                c.link(dve.tensor_tensor(gr(0), pl[:, :, 0:E], router_bias[:, :].unsqueeze(1).to_broadcast([P, T, E]), ALU.add))
                c.link(dve.tensor_reduce(gs_c[:, 0, :], gr(0), AX.X, ALU.max))
                dve.tensor_tensor(gr(1), gr(0), wide(0), ALU.subtract).then_inc(lg_here.sem, 1)
                ex_here(dve, b)
                at = 2
                for n in range(2):
                    c.link(dve.tensor_reduce(gs_c[:, 1 + n, :], gr(at), AX.X, ALU.max))
                    c.link(dve.tensor_tensor(gr(3), gr(at), wide(1 + n), ALU.is_equal))
                    c.link(dve.tensor_tensor(gr(4), gr(3), rmp, ALU.mult))
                    c.link(dve.tensor_reduce(gs_c[:, 3, :], gr(4), AX.X, ALU.max))
                    c.link(dve.tensor_tensor(gr(6 + n), gr(4), wide(3), ALU.is_equal))
                    if n == 0:
                        c.link(dve.scalar_tensor_tensor(gr(5), gr(6), -2.0, gr(2), ALU.mult, ALU.add))
                        at = 5
                c.link(dve.tensor_tensor(gr(8), gr(6), gr(7), ALU.add))
                c.link(dve.tensor_tensor(gr(9), gr(8), gr(2), ALU.mult))
                ins = dve.tensor_reduce(gs_c[:, 4, :], gr(9), AX.X, ALU.add)
                ins.then_inc(gate_sum.sem, 1); gate_sum(dve, b, 1)
                dve.reciprocal(gs_c[:, 5, :], gs_c[:, 4, :]).then_inc(gate_sum.sem, 1); gate_sum(dve, b, 2)
                dve.scalar_tensor_tensor(gr(10), gr(9), SCALING, wide(5), ALU.mult, ALU.mult).then_inc(gate_sum.sem, 1); gate_sum(dve, b, 3)
                gm_turn.before(dve, b)
                for t in range(T):
                    ins = dve.tensor_tensor(gm[:, t, :].rearrange("p (e r) -> p e r", e=E), pl[:, t, E:E + P].rearrange("p (e r) -> p e r", e=E),
                                            g_c[:, 10, t, :].unsqueeze(2).to_broadcast([P, E, R]), ALU.mult)
                ins.then_inc(gm_here.sem, 1)
                c.end()

            def c2(b):
                c = ch["c2"]; c.start(dve, b)
                x2_kept(dve, b)
                for t in range(T):
                    ff_full(dve, b, t + 1)
                    dve.tensor_tensor(z_c[:, t, :], bank(1 + t), z_c[:, t, :], ALU.add).then_inc(zc_here.sem, 1)
                zc_here(dve, b)
                norm_stats(c, z_c, mv_c, rs_c, 0, vc_here)
                c.end()
                norm_apply(b, z_c, mv_c, rs_c, 0, rc_here, z_c, y_here)

            of = lambda f, *n: lambda b: f(b, *n)
            of = lambda f, *n: lambda b: f(b, *n)
            run(dve, [(A, of(a1_t8, 0, (0, 1, 2))), (A, of(a1_nat, 1)), (A, of(a1_t8, 1, (0, 1))), (C_, c1),
                      (B, b1_v), (A, a1_state), (B, of(b1_k, 0)), (A, of(a1_t8, 1, (2,))), (B, of(b1_q, 0)), (B, of(b1_keep, 0)),
                      (B, of(b1_k, 1)), (B, of(b1_q, 1)), (B, of(b1_keep, 1)),
                      (A, of(a2_max, 0)), (B, of(b2, 0)), (B, of(b2, 1)), (B, of(b2, 2)), (B, of(b2, 3)), (A, of(a2_out, 0)),
                      (B, of(b2, 4)), (A, of(a2_max, 1)), (B, of(b2, 5)), (B, of(b2, 6)), (B, of(b2, 7)),
                      (B, b2_max), (A, of(a2_out, 1)), (A, a3), (NEXT, a0), (NEXT, a0_round), (C_, c2), (A, a3_z), (B, of(b3, 0)),
                      (A, a4_stats), (B, of(b3, 1)), (NEXT, of(a1_nat, 0, [0, 1])), (B, of(b4_z, 0)), (B, of(b4_z, 1)), (B, b4), (NEXT, of(a1_nat, 0, [2])), (B, b4_x2), (A, a4)])


_INS = ["x", "ctx_2048", "L0_attn_qkv_w", "L0_attn_qkv_b", "L0_attn_proj_w", "L0_attn_proj_b", "L0_attn_norm_w",
        "L0_xattn_Wq", "L0_xattn_Wk", "L0_xattn_Wv", "L0_xattn_Wsk", "L0_xattn_Wsv", "L0_xattn_Wo",
        "L0_ffn_base_w", "L0_ffn_base_b", "L0_ffn_router_w", "L0_ffn_router_b", "L0_ffn_lora_A", "L0_ffn_lora_B"]


def kernel(**inputs):
    import ml_dtypes
    import concourse.bacc as bacc
    from concourse.bass_utils import run_bass_kernel_spmd

    nc = bacc.Bacc("TRN2", target_bir_lowering=False, num_devices=1)
    (_, f_arr), (_, b_arr) = constants()
    arrays = {name: np.ascontiguousarray(inputs[name]) for name in _INS}
    arrays["const_f"] = f_arr
    arrays["const_b"] = b_arr.astype(ml_dtypes.bfloat16)
    d = {name: nc.dram_tensor(name, a.shape, mybir.dt.from_np(a.dtype), kind="ExternalInput").ap()
         for name, a in arrays.items()}
    out = nc.dram_tensor("y", (NB, N, C), F32, kind="ExternalOutput").ap()
    program(nc, d, out)
    r = run_bass_kernel_spmd(nc, [arrays], core_ids=[0])
    return r.results[0]["y"]
```
